# Optimizing a Trainium2 kernel written in Bass

```python
import numpy as np
import jax
import jax.numpy as jnp

def _softmax(x, axis=-1):
    return jax.nn.softmax(x, axis=axis)

def _gelu(x):
    return jax.nn.gelu(x, approximate=True)

def _silu(x):
    return jax.nn.silu(x)

def _sigmoid(x):
    return jax.nn.sigmoid(x)

def _layernorm(x, axis=-1, eps=1e-05):
    m = jnp.mean(x, axis=axis, keepdims=True)
    v = jnp.var(x, axis=axis, keepdims=True)
    return (x - m) / jnp.sqrt(v + eps)

def _scatter_add(tgt, idx, src, axis=0):
    return tgt.at[idx].add(src)

def _segment_sum(src, seg, n):
    return jax.ops.segment_sum(src, seg, n)
kernel_name = 'mk_conv_attn_hybrid_d2_conv_nchw256_r2_8e67aa'

def setup_inputs(seed: int=0):
    np.random.seed(seed)
    _w = jnp.asarray

    def _rec_inputs():
        import jax
        import jax.numpy as jnp
        _gk = jax.random.key(seed)
        x = -0.0005207 + 1.001 * jax.random.normal(jax.random.fold_in(_gk, 1), (2, 128, 32, 32), jnp.float32)
        return x
    x = _rec_inputs()

    def _L0_conv_setup():
        import jax, jax.numpy as jnp
        import numpy as np
        import math
        N_HEAD = 4
        NORM_GROUPS = 16
        EPS = 1e-05

        def _group_norm(x, weight, bias):
            B, C, H, W = x.shape
            g = x.reshape(B, NORM_GROUPS, C // NORM_GROUPS, H, W)
            mu = g.mean(axis=(2, 3, 4), keepdims=True)
            var = g.var(axis=(2, 3, 4), keepdims=True)
            g = (g - mu) * jax.lax.rsqrt(var + EPS)
            return g.reshape(B, C, H, W) * weight[:, None, None] + bias[:, None, None]
        key = jax.random.key(seed)
        ks = jax.random.split(key, 4)
        B, C, H, W = (2, 128, 32, 32)
        return {'input': jax.random.normal(ks[0], (B, C, H, W), dtype=jnp.float32), 'gn_weight': jnp.ones((C,), dtype=jnp.float32), 'gn_bias': jnp.zeros((C,), dtype=jnp.float32), 'qkv_weight': jax.random.normal(ks[1], (3 * C, C), dtype=jnp.float32) / math.sqrt(C), 'out_weight': jax.random.normal(ks[2], (C, C), dtype=jnp.float32) / math.sqrt(C), 'out_bias': jnp.zeros((C,), dtype=jnp.float32)}
    _L0_conv_all = _L0_conv_setup()
    _L0_conv_in = {k: v for k, v in _L0_conv_all.items() if k in ('gn_weight', 'gn_bias', 'qkv_weight', 'out_weight', 'out_bias')}
    del _L0_conv_all

    def _L1_attn_setup():
        import jax, jax.numpy as jnp
        import numpy as np
        import math
        N, HW, D = (8, 8192, 128)
        HEADS = 8
        key = jax.random.key(seed)
        ks = jax.random.split(key, 9)
        s = 1.0 / math.sqrt(D)
        return {'x': jax.random.normal(ks[0], (N, HW, D), jnp.float32), 'Wk': jax.random.normal(ks[1], (D, D), jnp.float32) * s, 'bk': jax.random.normal(ks[2], (D,), jnp.float32) * 0.01, 'Wq': jax.random.normal(ks[3], (D, D), jnp.float32) * s, 'bq': jax.random.normal(ks[4], (D,), jnp.float32) * 0.01, 'Wv': jax.random.normal(ks[5], (D, D), jnp.float32) * s, 'bv': jax.random.normal(ks[6], (D,), jnp.float32) * 0.01, 'Wr': jax.random.normal(ks[7], (D, D), jnp.float32) * s, 'br': jax.random.normal(ks[8], (D,), jnp.float32) * 0.01}
    _L1_attn_all = _L1_attn_setup()
    _L1_attn_in = {k: v for k, v in _L1_attn_all.items() if k in ('Wk', 'bk', 'Wq', 'bq', 'Wv', 'bv', 'Wr', 'br')}
    del _L1_attn_all

    def _L1_ffn_setup():
        import jax, jax.numpy as jnp
        import numpy as np
        TOP_K = 2
        LN_EPS = 1e-05
        key = jax.random.key(seed)
        ks = jax.random.split(key, 8)
        B, S, D, E, H = (16, 512, 128, 8, 512)
        x = jax.random.normal(ks[0], (B, S, D), dtype=jnp.float32)
        Wr = jax.random.normal(ks[1], (D, E), dtype=jnp.float32) * 0.1
        br = jnp.zeros((E,), dtype=jnp.float32)
        ln_g = jnp.ones((E, D), dtype=jnp.float32)
        ln_b = jnp.zeros((E, D), dtype=jnp.float32)
        W1 = jax.random.normal(ks[2], (E, D, H), dtype=jnp.float32) * (1.0 / np.sqrt(D))
        b1 = jnp.zeros((E, H), dtype=jnp.float32)
        W2 = jax.random.normal(ks[3], (E, H, D), dtype=jnp.float32) * (1.0 / np.sqrt(H))
        b2 = jnp.zeros((E, D), dtype=jnp.float32)
        return {'x': x, 'Wr': Wr, 'br': br, 'ln_g': ln_g, 'ln_b': ln_b, 'W1': W1, 'b1': b1, 'W2': W2, 'b2': b2}
    _L1_ffn_all = _L1_ffn_setup()
    _L1_ffn_in = {k: v for k, v in _L1_ffn_all.items() if k in ('Wr', 'br', 'ln_g', 'ln_b', 'W1', 'b1', 'W2', 'b2')}
    del _L1_ffn_all
    return {'x': x, 'L0_conv_gn_weight': _L0_conv_in['gn_weight'], 'L0_conv_gn_bias': _L0_conv_in['gn_bias'], 'L0_conv_qkv_weight': _L0_conv_in['qkv_weight'], 'L0_conv_out_weight': _L0_conv_in['out_weight'], 'L0_conv_out_bias': _L0_conv_in['out_bias'], 'L1_attn_Wk': _L1_attn_in['Wk'], 'L1_attn_bk': _L1_attn_in['bk'], 'L1_attn_Wq': _L1_attn_in['Wq'], 'L1_attn_bq': _L1_attn_in['bq'], 'L1_attn_Wv': _L1_attn_in['Wv'], 'L1_attn_bv': _L1_attn_in['bv'], 'L1_attn_Wr': _L1_attn_in['Wr'], 'L1_attn_br': _L1_attn_in['br'], 'L1_ffn_Wr': _L1_ffn_in['Wr'], 'L1_ffn_br': _L1_ffn_in['br'], 'L1_ffn_ln_g': _L1_ffn_in['ln_g'], 'L1_ffn_ln_b': _L1_ffn_in['ln_b'], 'L1_ffn_W1': _L1_ffn_in['W1'], 'L1_ffn_b1': _L1_ffn_in['b1'], 'L1_ffn_W2': _L1_ffn_in['W2'], 'L1_ffn_b2': _L1_ffn_in['b2']}

def reference(x, L0_conv_gn_weight, L0_conv_gn_bias, L0_conv_qkv_weight, L0_conv_out_weight, L0_conv_out_bias, L1_attn_Wk, L1_attn_bk, L1_attn_Wq, L1_attn_bq, L1_attn_Wv, L1_attn_bv, L1_attn_Wr, L1_attn_br, L1_ffn_Wr, L1_ffn_br, L1_ffn_ln_g, L1_ffn_ln_b, L1_ffn_W1, L1_ffn_b1, L1_ffn_W2, L1_ffn_b2):
    import jax
    import jax.numpy as jnp

    def _L0_conv_ref(input, gn_weight, gn_bias, qkv_weight, out_weight, out_bias):
        import jax, jax.numpy as jnp
        import numpy as np
        import math
        N_HEAD = 4
        NORM_GROUPS = 16
        EPS = 1e-05

        def _group_norm(x, weight, bias):
            B, C, H, W = x.shape
            g = x.reshape(B, NORM_GROUPS, C // NORM_GROUPS, H, W)
            mu = g.mean(axis=(2, 3, 4), keepdims=True)
            var = g.var(axis=(2, 3, 4), keepdims=True)
            g = (g - mu) * jax.lax.rsqrt(var + EPS)
            return g.reshape(B, C, H, W) * weight[:, None, None] + bias[:, None, None]
        B, C, H, W = input.shape
        head_dim = C // N_HEAD
        x = _group_norm(input, gn_weight, gn_bias)
        qkv = jnp.einsum('bchw,oc->bohw', x, qkv_weight)
        qkv = qkv.reshape(B, N_HEAD, 3 * head_dim, H, W)
        q, k, v = jnp.split(qkv, 3, axis=2)
        attn = jnp.einsum('bnchw,bncyx->bnhwyx', q, k) / math.sqrt(C)
        attn = jax.nn.softmax(attn.reshape(B, N_HEAD, H, W, H * W), axis=-1)
        attn = attn.reshape(B, N_HEAD, H, W, H, W)
        out = jnp.einsum('bnhwyx,bncyx->bnchw', attn, v).reshape(B, C, H, W)
        out = jnp.einsum('bchw,oc->bohw', out, out_weight) + out_bias[:, None, None]
        return out + input

    def _L1_attn_ref(x, Wk, bk, Wq, bq, Wv, bv, Wr, br):
        import jax, jax.numpy as jnp
        import numpy as np
        import math
        N, HW, D = (8, 8192, 128)
        HEADS = 8
        n, hw, d = x.shape
        heads = HEADS
        hk = d // heads
        hv = d // heads
        flat = x.reshape(n, d, hw)
        keys = jnp.einsum('kd,ndl->nkl', Wk, flat) + bk[None, :, None]
        queries = jnp.einsum('kd,ndl->nkl', Wq, flat) + bq[None, :, None]
        values = jnp.einsum('vd,ndl->nvl', Wv, flat) + bv[None, :, None]
        K = jax.nn.softmax(keys.reshape(n, heads, hk, hw), axis=3)
        Q = jax.nn.softmax(queries.reshape(n, heads, hk, hw), axis=2)
        V = values.reshape(n, heads, hv, hw)
        context = jnp.einsum('nhkl,nhvl->nhkv', K, V)
        att = jnp.einsum('nhkv,nhkl->nhvl', context, Q)
        agg = att.reshape(n, heads * hv, hw)
        out = jnp.einsum('dv,nvl->ndl', Wr, agg) + br[None, :, None]
        return out.reshape(n, hw, d)

    def _L1_ffn_ref(x, Wr, br, ln_g, ln_b, W1, b1, W2, b2):
        import jax, jax.numpy as jnp
        import numpy as np
        TOP_K = 2
        LN_EPS = 1e-05
        B, S, D = x.shape
        N = B * S
        xt = x.reshape(N, D)
        logits = xt @ Wr + br
        probs = jax.nn.softmax(logits, axis=-1)
        top_p, top_idx = jax.lax.top_k(probs, TOP_K)
        weights = top_p / top_p.sum(axis=-1, keepdims=True)
        mu = xt.mean(axis=-1, keepdims=True)
        var = ((xt - mu) ** 2).mean(axis=-1, keepdims=True)
        xn = (xt - mu) * jax.lax.rsqrt(var + LN_EPS)
        xe = xn[None, :, :] * ln_g[:, None, :] + ln_b[:, None, :]
        h = jax.nn.gelu(jnp.einsum('end,edh->enh', xe, W1) + b1[:, None, :], approximate=False)
        y = jnp.einsum('enh,ehd->end', h, W2) + b2[:, None, :]
        y_tok = jnp.transpose(y, (1, 0, 2))
        sel = jnp.take_along_axis(y_tok, top_idx[:, :, None], axis=1)
        out = (weights[:, :, None] * sel).sum(axis=1)
        return out.reshape(B, S, D)

    def _gn(v, G=32, eps=1e-05):
        B_, C_, H_, W_ = v.shape
        g = v.reshape(B_, G, C_ // G, H_, W_)
        m = jnp.mean(g, axis=(2, 3, 4), keepdims=True)
        s = jnp.var(g, axis=(2, 3, 4), keepdims=True)
        return ((g - m) / jnp.sqrt(s + eps)).reshape(v.shape)

    def _ln_c(v, eps=1e-06):
        m = jnp.mean(v, axis=1, keepdims=True)
        s = jnp.var(v, axis=1, keepdims=True)
        return (v - m) / jnp.sqrt(s + eps)

    def _ln_t(v, eps=1e-05):
        m = jnp.mean(v, axis=-1, keepdims=True)
        s = jnp.var(v, axis=-1, keepdims=True)
        return (v - m) / jnp.sqrt(s + eps)

    def _to_tokens(v):
        B_, C_, H_, W_ = v.shape
        return v.reshape(B_, C_, H_ * W_).transpose(0, 2, 1)

    def _from_tokens(t, like):
        B_, C_, H_, W_ = like.shape
        return t.transpose(0, 2, 1).reshape(B_, C_, H_, W_)
    x = _L0_conv_ref(x, L0_conv_gn_weight, L0_conv_gn_bias, L0_conv_qkv_weight, L0_conv_out_weight, L0_conv_out_bias)
    t = _to_tokens(x)
    t = t + _L1_attn_ref(_ln_t(t), L1_attn_Wk, L1_attn_bk, L1_attn_Wq, L1_attn_bq, L1_attn_Wv, L1_attn_bv, L1_attn_Wr, L1_attn_br)
    t = t + _L1_ffn_ref(_ln_t(t), L1_ffn_Wr, L1_ffn_br, L1_ffn_ln_g, L1_ffn_ln_b, L1_ffn_W1, L1_ffn_b1, L1_ffn_W2, L1_ffn_b2)
    x = _from_tokens(t, x)
    return x

_drawn_inputs = setup_inputs


def setup_inputs(seed=0):
    import zlib

    import numpy as np

    out = dict(_drawn_inputs(seed))
    spreads = {'L0_conv_gn_weight': (1.0, 0.2),
     'L0_conv_gn_bias': (0.0, 0.1),
     'L0_conv_out_bias': (0.0, 0.1),
     'L1_ffn_br': (0.0, 0.1),
     'L1_ffn_ln_g': (1.0, 0.2),
     'L1_ffn_ln_b': (0.0, 0.1),
     'L1_ffn_b1': (0.0, 0.1),
     'L1_ffn_b2': (0.0, 0.1)}
    factors = {'L1_attn_bk': 64.0, 'L1_attn_bq': 35.119, 'L1_attn_bv': 5.962, 'L1_attn_br': 6.179}
    for name, (base, spread) in spreads.items():
        noise = np.random.default_rng([zlib.crc32(name.encode()), seed]).standard_normal(out[name].shape)
        drawn = base * np.exp(spread * noise) if base else spread * noise
        out[name] = jnp.asarray(drawn.astype(out[name].dtype))
    for name, factor in factors.items():
        out[name] = (out[name] * factor).astype(out[name].dtype)
    return out
```

```python
import concourse.bass as bass
from concourse import mybir
from contextlib import ExitStack
from math import sqrt


def build_program(nc, x, gn_weight, gn_bias, qkv_weight, out_weight, out_bias, Wk, bk, Wq, bq, Wv, bv, Wr, br,
                  router_w, router_b, ln_g, ln_b, W1, b1, W2, b2, out):
    f32, f32r = mybir.dt.float32, mybir.dt.float32r
    i32, u32 = mybir.dt.int32, mybir.dt.uint32
    ALU, ACT, AX = mybir.AluOpType, mybir.ActivationFunctionType, mybir.AxisListType.X

    B, C, H_, W_ = x.shape
    L = H_ * W_
    P = 128
    J = L // P
    HALF = 512
    HEADS0, HD = 4, 32
    PAIRS = HEADS0 // 2
    UNITS = B * PAIRS
    QT, KT = L // P, L // P
    STEPS = 2 * KT
    SCORE_SCALE = 1.0 / sqrt(C)
    HEADS1, HK = 8, 16
    E, D, HID = W1.shape
    HC = HID // P
    TILES = (2 * L + E * (P - 1)) // P
    EPS = 1e-5
    SPLIT = 3 * HD
    STACK = SPLIT + 2
    RING = 2 * 2 * QT + 1

    xs = [nc.dram_tensor(f"expert_in_{b}", (TILES * P, D), f32).ap() for b in range(B)]
    ys = [nc.dram_tensor(f"expert_out_{b}", (TILES * P, D), f32).ap() for b in range(B)]

    ctx = ExitStack()
    with ctx:
        base = nc.sbuf_base
        room = [0]
        ctx.enter_context(nc.sbuf_tensor("slab", [P, 208 * 1024 - 512], mybir.dt.uint8))
        start = (base + 31) // 32 * 32

        def at(name, shape, dt, offset):
            size = 4
            for n in shape[1:]:
                size *= n
            return nc.alloc_sbuf_tensor_at(name, list(shape), dt, offset=start + offset), offset + size

        def sb(name, shape, dt=f32):
            t, end = at(name, shape, dt, room[0])
            room[0] = (end + 31) // 32 * 32
            return t

        def sem(name):
            return ctx.enter_context(nc.semaphore(name))

        w1 = sb("w1", [P, E, HID])
        bias1 = sb("bias1", [P, E, HID])
        w2 = sb("w2", [P, E, HC, D])
        bias2 = sb("bias2", [P, E, D])
        wT = sb("wT", [P, 8, P])
        vcol = sb("vcol", [P, 5 + 2 * E])
        bqv = sb("bqv", [P, 2, P])
        rw = sb("rw", [P, E])
        rb = sb("rb", [P, E])
        ident = sb("ident", [P, P])
        ones = sb("ones", [P, P])
        upper = sb("upper", [P, P])
        gmat = sb("gmat", [P, P])
        bmask = sb("bmask", [P, P])
        iota_e = sb("iota_e", [P, E])
        seg = sb("seg", [P, E, J])
        t_iota = sb("t_iota", [1, TILES, E])
        minus_half = sb("minus_half", [P, J])
        X = sb("X", [P, B, L])
        xn = sb("xn", [P, B, L])
        t2 = sb("t2", [P, B, J, P])
        X2 = sb("X2", [P, B, J, P])
        probs = sb("probs", [P, 3, 2 * HALF])
        vT = sb("vT", [P, B, KT, C])
        attn = sb("attn", [P, B, L])
        wrow = attn[:, 0, :].rearrange("p (j c) -> p j c", j=8)
        vrow = attn[0:5 + 2 * E, 1, 0:P]
        hl_at = room[0]
        q_hi, q_lo = sb("q_hi", [P, L], f32r), sb("q_lo", [P, L], f32r)
        k_hi, k_lo = sb("k_hi", [P, L], f32r), sb("k_lo", [P, L], f32r)
        stack_at = room[0]
        Qs = sb("Qs", [P, B, HEADS0, L], f32r)
        Ks = sb("Ks", [P, B, HEADS0, L], f32r)
        QV, o = at("QV", [P, J, 2, P], f32, hl_at)
        QT_sb, o = at("QT_sb", [P, L], f32, o)
        F, o = at("F", [P, J, P], f32, o)
        assert o <= stack_at
        EK, EKT = xn[:, 0, :], xn[:, 1, :].rearrange("p (j k) -> p j k", j=J)
        CT, M1 = xn[:, 0, 0:P], xn[:, 0, P:2 * P]
        tot, incl, slotv = (xn[:, 0, 2 * P + i * E * J:2 * P + (i + 1) * E * J].rearrange("p (e j) -> p e j", e=E)
                            for i in range(3))
        hot = xn[:, 0, 4 * P:4 * P + 2 * E * J].rearrange("p (w e j) -> p w e j", w=2, e=E)
        cmp = xn[0:1, 0, 5 * P:5 * P + TILES * E].rearrange("p (t e) -> p t e", e=E)
        XR, o = at("XR", [P, 2, P], f32, stack_at)
        XTT, o = at("XTT", [P, 2, P], f32, o)
        H1, o = at("H1", [P, 2, HID], f32, o)
        G, o = at("G", [P, 2, HID], f32, o)
        GT, o = at("GT", [P, 2, HC, P], f32, o)
        Y, o = at("Y", [P, 2, D], f32, o)
        YG, o = at("YG", [P, 2 * J, D], f32, o)
        OUT, o = at("OUT", [P, L], f32, o)
        assert o <= stack_at + 2 * B * HEADS0 * L * 4
        gst = sb("gst", [P, B, 2, 6])
        gmv = sb("gmv", [P, B, 2])
        gtmp = sb("gtmp", [P, B, 4])
        ve = sb("ve", [P, 2 + 3 * B, J])
        rstd = sb("rstd", [P, 2 + 3 * B, J])
        lst = sb("lst", [P, J, 6])
        lmv = sb("lmv", [P, J, 2])
        pm = sb("pm", [P, 2, QT, 2])
        negm = sb("negm", [P, 2, QT])
        mhl = sb("mhl", [P, 2, 2, QT], f32r)
        mrow = sb("mrow", [4 * QT, P], f32r)
        rec = sb("rec", [64, HALF])
        kneg = sb("kneg", [P, 2])
        ksum = sb("ksum", [P, 2])
        qst = sb("qst", [P, J, HEADS1, 3])
        lg = sb("lg", [P, J, E])
        lst2 = sb("lst2", [P, J, 4])
        top = sb("top", [P, J, 8])
        topi = sb("topi", [P, J, 8], u32)
        topf = sb("topf", [P, J, 2])
        wts = sb("wts", [P, B, J, 2])
        mask = sb("mask", [P, E, J])
        cnt_i = sb("cnt_i", [P, E], i32)
        cnt = sb("cnt", [P, 3, E])
        slotf = sb("slotf", [P, 2, J])
        slots = sb("slots", [P, B, 2, J], u32)
        tabf = sb("tabf", [1, TILES])
        tab = sb("tab", [1, B, TILES], i32)
        assert start + room[0] <= nc.sbuf_usable_end

        ps = ctx.enter_context(nc.psum_tensor("ps", [P, 8 * HALF], f32))

        def bank(i, n=1):
            return ps[:, i * HALF:(i + n) * HALF]

        ld_x = [sem(f"ld_x{b}") for b in range(B)]
        ld_wqkv, ld_w, ld_vec, ld_rows = sem("ld_wqkv"), sem("ld_w"), sem("ld_vec"), sem("ld_rows")
        ld_w1, ld_b1, ld_w2, ld_b2 = sem("ld_w1"), sem("ld_b1"), sem("ld_w2"), sem("ld_b2")
        stack_in = [sem(f"stack_in{u}") for u in range(UNITS)]
        mrow_in = [sem(f"mrow_in{u}") for u in range(UNITS)]
        ones_in, xs_zeroed = sem("ones_in"), sem("xs_zeroed")
        scattered = [sem(f"scattered{b}") for b in range(B)]
        gathered = [sem(f"gathered{b}") for b in range(B)]
        x_in = [sem("x_in_even"), sem("x_in_odd")]
        y_out = [sem("y_out_even"), sem("y_out_odd")]
        stored = sem("stored")
        dve_chain, pool_chain, act_chain = sem("dve_chain"), sem("pool_chain"), sem("act_chain")
        ident_ready, consts_ready = sem("ident_ready"), sem("consts_ready")
        wT_ready, wT_sb = sem("wT_ready"), sem("wT_sb")
        vcol_ready, vcol_sb = sem("vcol_ready"), sem("vcol_sb")
        bias_ready, bias_done, w1_scaled = sem("bias_ready"), sem("bias_done"), sem("w1_scaled")
        gn_in, gn_out = sem("gn_in"), sem("gn_out")
        var_ready, rstd_ready = sem("var_ready"), sem("rstd_ready")
        xn_ready, resid_ready = sem("xn_ready"), sem("resid_ready")
        qkv_ready, hi_ready, qk_split, v_sb = sem("qkv_ready"), sem("hi_ready"), sem("qk_split"), sem("v_sb")
        slot_ready, slot_used = sem("slot_ready"), sem("slot_used")
        mhl_ready, mrow_ready = sem("mhl_ready"), sem("mrow_ready")
        st_ready, exp_done, pv_done, o_used = sem("st_ready"), sem("exp_done"), sem("pv_done"), sem("o_used")
        proj_ready, t_sb, F_ready = sem("proj_ready"), sem("t_sb"), sem("F_ready")
        keys_ready, kneg_ready, ek_ready = sem("keys_ready"), sem("kneg_ready"), sem("ek_ready")
        qv_ready, qv_sb = sem("qv_ready"), sem("qv_sb")
        ekT_ready, ekT_sb = sem("ekT_ready"), sem("ekT_sb")
        qsub_ready, qexp_ready, qn_ready = sem("qsub_ready"), sem("qexp_ready"), sem("qn_ready")
        ctx_ready, ct_sb, m1_ready, m1_sb = sem("ctx_ready"), sem("ct_sb"), sem("m1_ready"), sem("m1_sb")
        qT_ready, qT_sb, att_ready, n2_ready = sem("qT_ready"), sem("qT_sb"), sem("att_ready"), sem("n2_ready")
        n2T_ready, n2T_sb, lg_ready = sem("n2T_ready"), sem("n2T_sb"), sem("lg_ready")
        lsub_ready, lexp_ready = sem("lsub_ready"), sem("lexp_ready")
        mask_ready, cum_ready, slots_ready, tab_ready = sem("mask_ready"), sem("cum_ready"), sem("slots_ready"), sem("tab_ready")
        x2_ready = sem("x2_ready")
        xT_ready, xT_sb, h_ready, h_sb = sem("xT_ready"), sem("xT_sb"), sem("h_ready"), sem("h_sb")
        g_ready, gT_ready, gT_sb = sem("g_ready"), sem("gT_ready"), sem("gT_sb")
        y_ready, y_sb = sem("y_ready"), sem("y_sb")
        mix_ready, outT_ready, out_sb = sem("mix_ready"), sem("outT_ready"), sem("out_sb")

        def head(u, hd):
            return 2 * (u % PAIRS) + hd

        LOOP_FROM, TURNS = 4, (TILES - 5) // 2
        LOOP_TO = LOOP_FROM + 2 * TURNS
        LAST = TILES + 2

        def parity(b, t):
            return (TILES * b + t) % 2

        def earlier(b, t, p):
            n = TILES * b + t
            return (n + 1 - p) // 2

        def expert_steps(engine, b, step):
            for s in range(LOOP_FROM):
                step(s, 0)
            with engine.Fori(0, TURNS) as turn:
                for s in range(LOOP_FROM, LOOP_FROM + 2):
                    step(s, turn)
            for s in range(LOOP_TO, LAST):
                step(s, 0)

        def is_tile(t):
            return 0 <= t < TILES

        block = ctx.enter_context(nc.Block())

        @block.sync
        def _(sp):
            sp.dma_start(X[:, 0, :], x[0].rearrange("c h w -> c (h w)")).then_inc(ld_x[0], 16)
            for n in range(HEADS0):
                src = qkv_weight[n * SPLIT:(n + 1) * SPLIT, :].rearrange("(s i) c -> i s c", s=3)
                sp.dma_start(wrow[n * HD:(n + 1) * HD, 0:3, :], src).then_inc(ld_wqkv, 16)
            rows = 0
            for v in (gn_weight, gn_bias, out_bias, bk, br):
                sp.dma_start(vrow[rows:rows + 1, :], v.rearrange("(a c) -> a c", a=1)).then_inc(ld_vec, 16)
                rows += 1
            for v in (ln_g, ln_b):
                sp.dma_start(vrow[rows:rows + E, :], v).then_inc(ld_vec, 16)
                rows += E
            for n, w in enumerate((out_weight, Wq, Wv, Wk, Wr)):
                sp.dma_start(wrow[:, 3 + n, :], w).then_inc(ld_w, 16)
            sp.dma_start(X[:, 1, :], x[1].rearrange("c h w -> c (h w)")).then_inc(ld_x[1], 16)
            sp.dma_start(w1[:, :, :], W1.rearrange("e d h -> d e h")).then_inc(ld_w1, 16)

            def stacks(u):
                b = u // PAIRS
                sp.wait_ge(hi_ready, 2 * b + 2)
                sp.wait_ge(qk_split, 2 * b + 2)
                for hd in range(2):
                    n = head(u, hd)
                    rows = slice(n * HD, (n + 1) * HD)
                    for st, parts in ((Qs, (q_hi, q_hi, q_lo)), (Ks, (k_hi, k_lo, k_hi))):
                        for r, part in enumerate(parts):
                            sp.dma_start(st[r * HD:(r + 1) * HD, b, n, :].bitcast(f32),
                                         part[rows, :].bitcast(f32)).then_inc(stack_in[u], 16)

            def max_rows(u):
                b = u // PAIRS
                sp.wait_ge(mrow_ready, u + 1)
                for hd in range(2):
                    sp.dma_start(Qs[SPLIT:STACK, b, head(u, hd), :].bitcast(f32).rearrange("s (t q) -> s t q", t=QT),
                                 mrow[hd * 2 * QT:(hd + 1) * 2 * QT, :].bitcast(f32)).then_inc(mrow_in[u], 16)

            sp.wait_ge(consts_ready, 1)
            sp.dma_start(Ks[SPLIT:STACK, :, :, :].bitcast(f32).rearrange("s b n (t q) -> s (b n t) q", q=P),
                         ones[:, :]).then_inc(ones_in, 16)
            stacks(0)
            stacks(1)
            stacks(2)
            stacks(3)
            for e in range(E):
                sp.dma_start(w2[:, e, :, :], W2[e].rearrange("(c p) d -> p c d", p=P)).then_inc(ld_w2, 16)
            for u in range(UNITS):
                max_rows(u)

            def expert_io(b):
                sp.wait_ge(scattered[b], 16 * 2 * J)

                def step(s, turn):
                    t = s + 2 * turn
                    if is_tile(s):
                        p = parity(b, s)
                        if TILES * b + s >= 2:
                            sp.wait_ge(xT_ready, TILES * b - 1 + t)
                        sp.dma_start(XR[:, p, :], xs[b][bass.ts(t, P), :]).then_inc(x_in[p], 16)
                    if is_tile(s - 3):
                        p = parity(b, s - 3)
                        sp.wait_ge(y_sb, TILES * b + t - 2)
                        sp.dma_start(ys[b][bass.ts(t - 3, P), :], Y[:, p, :]).then_inc(y_out[p], 16)

                for s in range(3):
                    step(s, 0)
                with sp.Fori(0, (TILES - 3) // 2) as turn:
                    for s in (3, 4):
                        step(s, turn)
                for s in range(3 + 2 * ((TILES - 3) // 2), TILES + 3):
                    step(s, 0)

            for b in range(B):
                expert_io(b)
            for b in range(B):
                sp.wait_ge(out_sb, b + 1)
                sp.dma_start(out[b].rearrange("c h w -> c (h w)"), OUT[:, :]).then_inc(stored, 16)
                sp.wait_ge(stored, 16 * (b + 1))

        @block.gpsimd
        def _(pool):
            chain = [0]

            def link(ins):
                chain[0] += 1
                ins.then_inc(pool_chain, 1)
                pool.wait_ge(pool_chain, chain[0])

            def select(t, pattern, base_, mult, op, fill):
                link(nc.gpsimd.affine_select(out=t, in_=t, compare_op=op, fill=fill, base=base_, pattern=pattern,
                                             channel_multiplier=mult))

            link(nc.gpsimd.memset(ident[:, :], 0.0))
            select(ident[:, :], [[-1, P]], 0, 1, ALU.not_equal, 1.0)
            nc.gpsimd.memset(minus_half[:, :], -0.5).then_inc(ident_ready, 1)

            def blocks(t, value, size):
                link(nc.gpsimd.memset(t[:, :], value))
                v = t[:, :].rearrange("p (g i) -> p g i", i=size)
                select(v, [[-size, P // size], [0, size]], 0, 1, ALU.is_ge, 0.0)
                select(v, [[size, P // size], [0, size]], size - 1, -1, ALU.is_ge, 0.0)

            blocks(gmat, 1.0 / 8, 8)
            nc.gpsimd.memset(ones[:, :], 1.0).then_inc(consts_ready, 1)

            def rsqrt(i):
                n = 1 if i < B else J
                pool.wait_ge(var_ready, i + 1)
                nc.gpsimd.tensor_tensor(rstd[:, i, 0:n], ve[:, i, 0:n], minus_half[:, 0:n], ALU.pow).then_inc(rstd_ready, 1)

            rsqrt(0)
            rsqrt(1)
            blocks(bmask, 1.0, HK)
            link(nc.gpsimd.memset(upper[:, :], 1.0))
            select(upper[:, :], [[1, P]], 0, -1, ALU.is_gt, 0.0)
            nc.gpsimd.iota(iota_e[:, :], [[1, E]], base=0, channel_multiplier=0,
                           allow_small_or_imprecise_dtypes=True)
            nc.gpsimd.iota(t_iota[:, :, :], [[P, TILES], [0, E]], base=0, channel_multiplier=0,
                           allow_small_or_imprecise_dtypes=True)
            link(nc.gpsimd.memset(seg[:, :, :], 1.0))
            nc.gpsimd.memset(seg[:, :, 0:1], 0.0).then_inc(consts_ready, 1)
            link(nc.gpsimd.memset(X2[:, :, :, :], 0.0))
            zeros = X2[:, :, :, :].rearrange("p b j d -> p (b j d)")
            per = TILES * D // 2
            for b in range(B):
                v = xs[b].rearrange("(p r) d -> p (r d)", p=P)
                for i in range(2):
                    pool.dma_start(v[:, i * per:(i + 1) * per], zeros[:, 0:per]).then_inc(xs_zeroed, 16)
            pool.wait_ge(xs_zeroed, 16 * 2 * B)

            def scatter(b):
                pool.wait_ge(slots_ready, b + 1)
                pool.wait_ge(x2_ready, b + 1)
                for j in range(J):
                    for w in range(2):
                        pool.indirect_dma_start(xs[b][:, :], bass.IndirectOffsetOnAxis(ap=slots[:, b, w, j:j + 1], axis=0),
                                                X2[:, b, j, :], None).then_inc(scattered[b], 16)

            def gather(b):
                for p in range(2):
                    pool.wait_ge(y_out[p], 16 * earlier(b, TILES, p))
                if b:
                    pool.wait_ge(mix_ready, b)
                for j in range(J):
                    for w in range(2):
                        pool.indirect_dma_start(YG[:, 2 * j + w, :], None, ys[b][:, :],
                                                bass.IndirectOffsetOnAxis(ap=slots[:, b, w, j:j + 1], axis=0)
                                                ).then_inc(gathered[b], 16)

            for b in range(B):
                for i in range(3):
                    rsqrt(B + 3 * b + i)
                scatter(b)
            for b in range(B):
                gather(b)

        @block.scalar
        def _(act):
            act.dma_start(bqv[:, 0, :], bq.rearrange("(a c) -> a c", a=1).broadcast_to([P, P])).then_inc(ld_rows, 16)
            act.dma_start(bqv[:, 1, :], bv.rearrange("(a c) -> a c", a=1).broadcast_to([P, P])).then_inc(ld_rows, 16)
            act.dma_start(rb[:, :], router_b.rearrange("(a c) -> a c", a=1).broadcast_to([P, E])).then_inc(ld_rows, 16)
            act.dma_start(rw[:, :], router_w).then_inc(ld_rows, 16)
            act.dma_start(bias1[:, :, :].rearrange("p e h -> p (e h)"),
                          b1.rearrange("(a e) h -> a (e h)", a=1).broadcast_to([P, E * HID])).then_inc(ld_b1, 16)
            act.dma_start(bias2[:, :, :].rearrange("p e h -> p (e h)"),
                          b2.rearrange("(a e) h -> a (e h)", a=1).broadcast_to([P, E * D])).then_inc(ld_b2, 16)
            act.wait_ge(wT_ready, 1)
            nc.scalar.activation(wT[:, 0:4, :], ps[:, 0:4 * P].rearrange("p (j c) -> p j c", j=4), ACT.Copy)
            nc.scalar.activation(wT[:, 4:8, :], ps[:, 4 * P:8 * P].rearrange("p (j c) -> p j c", j=4),
                                 ACT.Copy).then_inc(wT_sb, 1)

            def split(b):
                act.wait_ge(qkv_ready, 3 * b + 1)
                if b:
                    for u in range(PAIRS):
                        act.wait_ge(stack_in[u], 16 * 12)
                nc.scalar.activation(q_hi[:, :], bank(4, 2), ACT.Copy, scale=SCORE_SCALE).then_inc(hi_ready, 1)
                act.wait_ge(qkv_ready, 3 * b + 2)
                nc.scalar.activation(k_hi[:, :], bank(6, 2), ACT.Copy).then_inc(hi_ready, 1)
                act.wait_ge(qkv_ready, 3 * b + 3)
                nc.scalar.activation(vT[:, b, :, :].rearrange("p t c -> p (t c)"), bank(2, 2), ACT.Copy).then_inc(v_sb, 1)

            def exps(u, step):
                s = u * STEPS + step
                act.wait_ge(st_ready, s + 1)
                if s >= 3:
                    act.wait_ge(pv_done, s - 2)
                nc.scalar.activation(probs[:, s % 3, :], bank(2 + 2 * (s % 2), 2), ACT.Exp).then_inc(exp_done, 1)

            def a_tokens(b):
                act.wait_ge(proj_ready, b + 1)
                nc.scalar.activation(t2[:, b, :, :].rearrange("p j c -> p (j c)"), bank(0, 2), ACT.Copy).then_inc(t_sb, 1)

            def a_key_exp(b):
                act.wait_ge(kneg_ready, b + 1)
                nc.scalar.activation(EK, bank(0, 2), ACT.Exp, bias=kneg[:, 1:2],
                                     accum_out=ksum[:, 0:1]).then_inc(ek_ready, 1)

            def a_keyT(b):
                act.wait_ge(ekT_ready, b + 1)
                nc.scalar.activation(xn[:, 1, :], bank(0, 2), ACT.Copy).then_inc(ekT_sb, 1)

            def a_query_exp(b):
                act.wait_ge(qsub_ready, b + 1)
                q = QV[:, :, 0, :]
                nc.scalar.activation(q, q, ACT.Exp).then_inc(qexp_ready, 1)

            def a_queryT(b):
                act.wait_ge(qT_ready, b + 1)
                nc.scalar.activation(QT_sb[:, :], bank(0, 2), ACT.Copy).then_inc(qT_sb, 1)

            def a_tokenT(b):
                act.wait_ge(n2T_ready, b + 1)
                nc.scalar.activation(QT_sb[:, :], bank(0, 2), ACT.Copy).then_inc(n2T_sb, 1)

            def a_route(b):
                act.wait_ge(lsub_ready, b + 1)
                nc.scalar.activation(lg[:, :, :], lg[:, :, :], ACT.Exp).then_inc(lexp_ready, 1)

            layer1 = [a_tokens, a_key_exp, a_keyT, a_query_exp, a_queryT, a_tokenT, a_route]

            split(0)
            split(1)
            for u in range(UNITS):
                for step in range(STEPS):
                    exps(u, step)
            for b in range(B):
                for part in layer1:
                    part(b)

            def experts(b):
                def step(s, turn):
                    n = TILES * b + s + 2 * turn
                    if is_tile(s):
                        p = parity(b, s)
                        act.wait_ge(h_sb, n + 1)
                        if TILES * b + s >= 2:
                            act.wait_ge(gT_ready, n - 1)
                        nc.scalar.activation(G[:, p, :], H1[:, p, :], ACT.Gelu).then_inc(g_ready, 1)
                    if is_tile(s - 1):
                        p = parity(b, s - 1)
                        act.wait_ge(gT_ready, n)
                        if TILES * b + s >= 3:
                            act.wait_ge(y_ready, n - 2)
                        nc.scalar.activation(GT[:, p, :, :].rearrange("p c t -> p (c t)"), bank(3 + p),
                                             ACT.Copy).then_inc(gT_sb, 1)

                expert_steps(act, b, step)

            for b in range(B):
                experts(b)
            for b in range(B):
                act.wait_ge(outT_ready, b + 1)
                if b:
                    act.wait_ge(stored, 16 * b)
                v = OUT[:, :].rearrange("c (d j) -> c d j", j=J)
                nc.scalar.activation(v, ps[:, 0:L].rearrange("c (j d) -> c d j", j=J), ACT.Copy).then_inc(out_sb, 1)

        @block.tensor
        def _(pe):
            pe.wait_ge(ident_ready, 1)
            pe.wait_ge(ld_vec, 16 * 7)
            n = 5 + 2 * E
            nc.tensor.transpose(ps[:, 2 * HALF:2 * HALF + n], vrow, ident[0:n, 0:n]).then_inc(vcol_ready, 1)
            pe.wait_ge(ld_wqkv, 16 * HEADS0)
            pe.wait_ge(ld_w, 16 * 5)
            for j in range(8):
                last = nc.tensor.transpose(ps[:, j * P:(j + 1) * P], wrow[:, j, :], ident[:, :])
            last.then_inc(wT_ready, 1)

            def group_stats(b):
                for i in range(2):
                    pe.wait_ge(gn_in, 2 * b + i + 1)
                    if not (b or i):
                        pe.wait_ge(consts_ready, 1)
                        pe.wait_ge(wT_sb, 1)
                    src = gmv[:, b, 0:1] if i == 0 else gtmp[:, b, 1:2]
                    nc.tensor.matmul(ps[:, HALF + 2 * b + i:HALF + 2 * b + i + 1], gmat[:, :], src,
                                     start=True, stop=True).then_inc(gn_out, 1)

            def qkv(b):
                pe.wait_ge(xn_ready, b + 1)
                if b == 0:
                    pe.wait_ge(vcol_sb, 1)
                for i, at_ in ((0, 4), (1, 6)):
                    if b:
                        pe.wait_ge(qk_split, i + 1)
                    for h in range(2):
                        last = nc.tensor.matmul(bank(at_ + h), wT[:, i, :], xn[:, b, h * HALF:(h + 1) * HALF],
                                                start=True, stop=True)
                    last.then_inc(qkv_ready, 1)
                if b:
                    pe.wait_ge(v_sb, b)
                for t in range(KT):
                    last = nc.tensor.matmul(ps[:, 2 * HALF + t * P:2 * HALF + (t + 1) * P],
                                            xn[:, b, t * P:(t + 1) * P], wT[:, 2, :], start=True, stop=True)
                last.then_inc(qkv_ready, 1)

            def max_slot(u, i):
                g = u * RING + i
                b = u // PAIRS
                if i == 0:
                    pe.wait_ge(stack_in[u], 16 * 12)
                if g >= 2:
                    pe.wait_ge(slot_used, g - 1)
                elif g == 1:
                    pe.wait_ge(var_ready, B)
                if i < RING - 1:
                    hd, t, h = i // (2 * QT), (i // 2) % QT, i % 2
                    n = head(u, hd)
                    last = nc.tensor.matmul(bank(g % 2), Qs[0:SPLIT, b, n, t * P:(t + 1) * P],
                                            Ks[0:SPLIT, b, n, h * HALF:(h + 1) * HALF], start=True, stop=True)
                else:
                    pe.wait_ge(mhl_ready, u + 1)
                    last = nc.tensor.transpose(ps[0:4 * QT, (g % 2) * HALF:(g % 2) * HALF + P],
                                               mhl[:, :, :, :].bitcast(f32).rearrange("p h s t -> p (h s t)"), ident[:, :])
                last.then_inc(slot_ready, 1)

            def scores(u, step):
                s = u * STEPS + step
                b, qh, kt = u // PAIRS, step // KT, step % KT
                if step == 0:
                    pe.wait_ge(mrow_in[u], 16 * 2)
                if s >= 2:
                    pe.wait_ge(exp_done, s - 1)
                else:
                    pe.wait_ge(v_sb, B)
                    pe.wait_ge(qk_split, 2 * B)
                    pe.wait_ge(ones_in, 16)
                for hd in range(2):
                    n = head(u, hd)
                    last = nc.tensor.matmul(bank(2 + 2 * (s % 2) + hd), Ks[0:STACK, b, n, kt * P:(kt + 1) * P],
                                            Qs[0:STACK, b, n, qh * HALF:(qh + 1) * HALF], start=True, stop=True)
                last.then_inc(st_ready, 1)

            def values(u, step):
                s = u * STEPS + step
                b, qh, kt = u // PAIRS, step // KT, step % KT
                o = 2 * u + qh
                pe.wait_ge(exp_done, s + 1)
                if kt == 0 and o >= 2:
                    pe.wait_ge(o_used, o - 1)
                for i in range(4):
                    n = head(u, i % 2)
                    w = vT[:, b, kt, n * HD:(n + 1) * HD] if i < 2 else ones[:, 0:HD]
                    last = nc.tensor.matmul(bank(6 + o % 2)[i * HD:(i + 1) * HD, :], w,
                                            probs[:, s % 3, (i % 2) * HALF:(i % 2 + 1) * HALF],
                                            start=kt == 0, stop=kt == KT - 1)
                last.then_inc(pv_done, 1)

            def t_project(b):
                pe.wait_ge(o_used, 4 * b + 4)
                pe.wait_ge(resid_ready, b + 1)
                if b:
                    pe.wait_ge(slots_ready, b)
                else:
                    pe.wait_ge(slot_used, UNITS * RING)
                for j in range(J):
                    o = ps[:, j * P:(j + 1) * P]
                    nc.tensor.matmul(o, attn[:, b, j::J], wT[:, 3, :], start=True, stop=False)
                    last = nc.tensor.matmul(o, X[:, b, j::J], ident[:, :], start=False, stop=True)
                last.then_inc(proj_ready, 1)

            def t_keys(b):
                pe.wait_ge(F_ready, b + 1)
                for h in range(2):
                    last = nc.tensor.matmul(bank(h), wT[:, 6, :], F[:, 4 * h:4 * h + 4, :].rearrange("d j c -> d (j c)"),
                                            start=True, stop=True)
                last.then_inc(keys_ready, 1)

            def t_query_value(b):
                pe.wait_ge(ek_ready, b + 1)
                for h in range(2):
                    if h:
                        pe.wait_ge(qv_sb, 2 * b + h)
                    for i in range(J // 2):
                        last = nc.tensor.matmul(ps[:, i * 2 * P:(i + 1) * 2 * P], F[:, 4 * h + i, :],
                                                wT[:, 4:6, :].rearrange("d w k -> d (w k)"), start=True, stop=True)
                    last.then_inc(qv_ready, 1)

            def t_keyT(b):
                pe.wait_ge(qv_sb, 2 * b + 2)
                for j in range(J):
                    last = nc.tensor.transpose(ps[:, j * P:(j + 1) * P], EK[:, j * P:(j + 1) * P], ident[:, :])
                last.then_inc(ekT_ready, 1)

            def t_context(b):
                pe.wait_ge(ekT_sb, b + 1)
                for j in range(J):
                    last = nc.tensor.matmul(ps[:, 0:P], QV[:, j, 1, :], EKT[:, j, :], start=j == 0, stop=j == J - 1)
                last.then_inc(ctx_ready, 1)
                pe.wait_ge(ct_sb, b + 1)
                nc.tensor.matmul(ps[:, HALF:HALF + P], CT, wT[:, 7, :], start=True, stop=True).then_inc(m1_ready, 1)

            def t_queryT(b):
                pe.wait_ge(qn_ready, b + 1)
                pe.wait_ge(m1_sb, b + 1)
                for j in range(J):
                    last = nc.tensor.transpose(ps[:, j * P:(j + 1) * P], QV[:, j, 0, :], ident[:, :])
                last.then_inc(qT_ready, 1)

            def t_attend(b):
                pe.wait_ge(qT_sb, b + 1)
                for h in range(2):
                    last = nc.tensor.matmul(bank(h), M1, QT_sb[:, h * HALF:(h + 1) * HALF], start=True, stop=True)
                last.then_inc(att_ready, 1)

            def t_tokenT(b):
                pe.wait_ge(n2_ready, b + 1)
                for j in range(J):
                    last = nc.tensor.transpose(ps[:, j * P:(j + 1) * P], F[:, j, :], ident[:, :])
                last.then_inc(n2T_ready, 1)

            def t_logits(b):
                pe.wait_ge(n2T_sb, b + 1)
                for j in range(J):
                    last = nc.tensor.matmul(ps[:, j * E:(j + 1) * E], QT_sb[:, j * P:(j + 1) * P], rw[:, :],
                                            start=True, stop=True)
                last.then_inc(lg_ready, 1)

            def t_counts(b):
                pe.wait_ge(mask_ready, b + 1)
                m = mask[:, :, :].rearrange("p e j -> p (e j)")
                nc.tensor.matmul(ps[:, HALF:HALF + E * J], upper[:, :], m, start=True, stop=True)
                nc.tensor.matmul(ps[:, HALF + E * J:HALF + 2 * E * J], ones[:, :], m, start=True,
                                 stop=True).then_inc(cum_ready, 1)

            layer1 = [t_project, t_keys, t_query_value, t_keyT, t_context, t_queryT, t_attend, t_tokenT, t_logits, t_counts]

            def expert_bias():
                pe.wait_ge(ld_w1, 16)
                for e in range(E):
                    pe.wait_ge(bias_ready, e + 1)
                    nc.tensor.matmul(bank(e % 2 + 6), H1[:, e % 2, 0:P], w1[:, e, :], start=True,
                                     stop=True).then_inc(bias_done, 1)

            group_stats(0)
            qkv(0)
            group_stats(1)
            qkv(1)
            for i in range(RING):
                max_slot(0, i)
            for u in range(UNITS):
                scores(u, 0)
                for step in range(STEPS):
                    if step + 1 < STEPS:
                        scores(u, step + 1)
                    if u + 1 < UNITS:
                        for i in range(2 * step, 2 * step + 2):
                            max_slot(u + 1, i)
                    values(u, step)
                if u + 1 < UNITS:
                    max_slot(u + 1, RING - 1)
            for b in range(B):
                pe.wait_ge(consts_ready, 2)
                if b == 0:
                    pe.wait_ge(ld_rows, 16 * 4)
                for part in layer1:
                    part(b)
            pe.wait_ge(o_used, 2 * UNITS)
            expert_bias()

            def experts(b):
                def x_transpose(s, turn):
                    p = parity(b, s)
                    n = TILES * b + s + 2 * turn
                    pe.wait_ge(x_in[p], 16 * (earlier(b, s, p) + 1 + turn))
                    if b == 0 and s == 0:
                        pe.wait_ge(slots_ready, B)
                    if TILES * b + s >= 2:
                        pe.wait_ge(xT_sb, n - 1)
                    nc.tensor.transpose(ps[:, p * P:(p + 1) * P], XR[:, p, :], ident[:, :]).then_inc(xT_ready, 1)

                def step(s, turn):
                    n = TILES * b + s + 2 * turn
                    if s == 0:
                        x_transpose(0, 0)
                    if is_tile(s):
                        p = parity(b, s)
                        e = pe.value_load(tab[0:1, b, bass.ds(s + 2 * turn, 1)], min_val=0, max_val=E - 1)
                        pe.wait_ge(xT_sb, n + 1)
                        if TILES * b + s >= 2:
                            pe.wait_ge(h_sb, n - 1)
                        nc.tensor.matmul(bank(1 + p), XTT[:, p, :], w1[:, e, :], start=True, stop=True).then_inc(h_ready, 1)
                    if is_tile(s - 1):
                        p = parity(b, s - 1)
                        pe.wait_ge(g_ready, n)
                        if TILES * b + s >= 3:
                            pe.wait_ge(gT_sb, n - 2)
                        for c in range(HC):
                            last = nc.tensor.transpose(ps[:, (3 + p) * HALF + c * P:(3 + p) * HALF + (c + 1) * P],
                                                       G[:, p, c * P:(c + 1) * P], ident[:, :])
                        last.then_inc(gT_ready, 1)
                    if is_tile(s + 1):
                        x_transpose(s + 1, turn)
                    if is_tile(s - 2):
                        p = parity(b, s - 2)
                        e = pe.value_load(tab[0:1, b, bass.ds(s - 2 + 2 * turn, 1)], min_val=0, max_val=E - 1)
                        pe.wait_ge(gT_sb, n - 1)
                        if TILES * b + s >= 4:
                            pe.wait_ge(y_sb, n - 3)
                        for c in range(HC):
                            last = nc.tensor.matmul(ps[:, (5 + p) * HALF:(5 + p) * HALF + D], GT[:, p, c, :],
                                                    w2[:, e, c, :], start=c == 0, stop=c == HC - 1)
                        last.then_inc(y_ready, 1)

                if b == 0:
                    pe.wait_ge(w1_scaled, 1)
                    pe.wait_ge(ld_w2, 16 * E)
                pe.wait_ge(tab_ready, b + 1)
                expert_steps(pe, b, step)

            for b in range(B):
                experts(b)
            for b in range(B):
                pe.wait_ge(mix_ready, b + 1)
                if b:
                    pe.wait_ge(out_sb, b)
                for j in range(J):
                    last = nc.tensor.transpose(ps[:, j * P:(j + 1) * P], t2[:, b, j, :], ident[:, :])
                last.then_inc(outT_ready, 1)

        @block.vector
        def _(dve):
            chain = [0]

            def link(ins):
                chain[0] += 1
                ins.then_inc(dve_chain, 1)
                dve.wait_ge(dve_chain, chain[0])

            dve.wait_ge(vcol_ready, 1)
            nc.vector.tensor_copy(vcol[:, :], ps[:, 2 * HALF:2 * HALF + 5 + 2 * E]).then_inc(vcol_sb, 1)
            dve.wait_ge(vcol_sb, 1)
            gn_w, gn_b, out_b, bk_c, br_c = (vcol[:, i:i + 1] for i in range(5))

            def group_norm(b):
                dve.wait_ge(ld_x[b], 16)
                for h in range(2):
                    last = nc.vector.bn_stats(gst[:, b, h, :], X[:, b, h * HALF:(h + 1) * HALF])
                link(last)
                nc.vector.bn_aggr(gmv[:, b, :], gst[:, b, :, :]).then_inc(gn_in, 1)
                dve.wait_ge(gn_out, 2 * b + 1)
                gm = gtmp[:, b, 2:3]
                link(nc.vector.tensor_copy(gm, ps[:, HALF + 2 * b:HALF + 2 * b + 1]))
                d = gtmp[:, b, 0:1]
                link(nc.vector.tensor_tensor(d, gmv[:, b, 0:1], gm, ALU.subtract))
                nc.vector.scalar_tensor_tensor(gtmp[:, b, 1:2], d, d, gmv[:, b, 1:2], ALU.mult, ALU.add).then_inc(gn_in, 1)
                dve.wait_ge(gn_out, 2 * b + 2)
                nc.vector.tensor_scalar_add(ve[:, b, 0:1], ps[:, HALF + 2 * b + 1:HALF + 2 * b + 2],
                                            EPS).then_inc(var_ready, 1)
                dve.wait_ge(rstd_ready, b + 1)
                sc = gtmp[:, b, 0:1]
                link(nc.vector.tensor_tensor(sc, rstd[:, b, 0:1], gn_w, ALU.mult))
                link(nc.vector.scalar_tensor_tensor(gtmp[:, b, 3:4], gm, sc, gn_b, ALU.mult, ALU.subtract))
                nc.vector.tensor_scalar(xn[:, b, :], X[:, b, :], sc, gtmp[:, b, 3:4], ALU.mult,
                                        ALU.subtract).then_inc(xn_ready, 1)
                dve.wait_ge(xn_ready, b + 1)
                nc.vector.tensor_scalar_add(X[:, b, :], X[:, b, :], out_b).then_inc(resid_ready, 1)

            def split(b):
                dve.wait_ge(hi_ready, 2 * b + 1)
                nc.vector.scalar_tensor_tensor(q_lo[:, :], bank(4, 2), SCORE_SCALE, q_hi[:, :].bitcast(f32), ALU.mult,
                                               ALU.subtract).then_inc(qk_split, 1)
                dve.wait_ge(hi_ready, 2 * b + 2)
                nc.vector.tensor_tensor(k_lo[:, :], bank(6, 2), k_hi[:, :].bitcast(f32), ALU.subtract).then_inc(qk_split, 1)

            def max_slot(u, i):
                g = u * RING + i
                if i < RING - 1:
                    hd, t, h = i // (2 * QT), (i // 2) % QT, i % 2
                    dve.wait_ge(slot_ready, g + 1)
                    nc.vector.tensor_reduce(pm[:, hd, t, h:h + 1], bank(g % 2), AX, ALU.max).then_inc(slot_used, 1)
                    return
                dve.wait_ge(slot_used, g)
                link(nc.vector.tensor_reduce(negm[:, :, :], pm[:, :, :, :], AX, ALU.max, negate=True))
                link(nc.vector.tensor_copy(mhl[:, :, 0, :], negm[:, :, :]))
                nc.vector.tensor_tensor(mhl[:, :, 1, :], negm[:, :, :], mhl[:, :, 0, :].bitcast(f32),
                                        ALU.subtract).then_inc(mhl_ready, 1)
                dve.wait_ge(slot_ready, g + 1)
                if u:
                    dve.wait_ge(mrow_in[u - 1], 16 * 2)
                nc.vector.tensor_copy(mrow[:, :], ps[0:4 * QT, (g % 2) * HALF:(g % 2) * HALF + P]).then_inc(mrow_ready, 1)
                dve.wait_ge(mrow_ready, u + 1)
                nc.vector.nop().then_inc(slot_used, 1)

            def normalise(u, qh):
                o = 2 * u + qh
                b, pair = u // PAIRS, u % PAIRS
                dve.wait_ge(pv_done, u * STEPS + (qh + 1) * KT)
                if o:
                    dve.wait_ge(o_used, o)
                link(nc.vector.reciprocal(rec[:, :], bank(6 + o % 2)[64:128, :]))
                nc.vector.tensor_tensor(attn[64 * pair:64 * pair + 64, b, qh * HALF:(qh + 1) * HALF],
                                        bank(6 + o % 2)[0:64, :], rec[:, :], ALU.mult).then_inc(o_used, 1)

            def layer_norm(src, dst, i, done=None):
                for j in range(J):
                    last = nc.vector.bn_stats(lst[:, j, :], src[:, j, :])
                link(last)
                for j in range(J):
                    last = nc.vector.bn_aggr(lmv[:, j, :], lst[:, j, :])
                link(last)
                nc.vector.tensor_scalar_add(ve[:, i, :], lmv[:, :, 1], EPS).then_inc(var_ready, 1)
                dve.wait_ge(rstd_ready, i + 1)
                for j in range(J):
                    last = nc.vector.tensor_scalar(dst[:, j, :], src[:, j, :], lmv[:, j, 0:1], rstd[:, i, j:j + 1],
                                                   ALU.subtract, ALU.mult)
                last.then_inc(done, 1)

            def v_tokens(b):
                dve.wait_ge(t_sb, b + 1)
                layer_norm(t2[:, b, :, :], F, B + 3 * b, F_ready)

            def v_key_max(b):
                dve.wait_ge(keys_ready, b + 1)
                link(nc.vector.tensor_reduce(kneg[:, 0:1], bank(0, 2), AX, ALU.max, negate=True))
                nc.vector.tensor_scalar(kneg[:, 1:2], kneg[:, 0:1], bk_c, bk_c, ALU.subtract, ALU.add).then_inc(kneg_ready, 1)

            def v_query_value(b):
                for h in range(2):
                    dve.wait_ge(qv_ready, 2 * b + h + 1)
                    nc.vector.tensor_tensor(QV[:, 4 * h:4 * h + 4, :, :].rearrange("p j w k -> p j (w k)"),
                                            bank(0, 2).rearrange("p (j k) -> p j k", j=4),
                                            bqv[:, :, :].rearrange("p w k -> p (w k)").unsqueeze(1).broadcast_to([P, 4, 2 * P]),
                                            ALU.add).then_inc(qv_sb, 1)

            def v_query_softmax(b):
                dve.wait_ge(qv_sb, 2 * b + 2)
                q = QV[:, :, 0, :].rearrange("p j (h k) -> p j h k", k=HK)

                def spread(i):
                    return qst[:, :, :, i].unsqueeze(3).broadcast_to([P, J, HEADS1, HK])

                link(nc.vector.tensor_reduce(qst[:, :, :, 0], q, AX, ALU.max))
                nc.vector.tensor_tensor(q, q, spread(0), ALU.subtract).then_inc(qsub_ready, 1)
                dve.wait_ge(qexp_ready, b + 1)
                link(nc.vector.tensor_reduce(qst[:, :, :, 1], q, AX, ALU.add))
                link(nc.vector.reciprocal(qst[:, :, :, 2], qst[:, :, :, 1]))
                nc.vector.tensor_tensor(q, q, spread(2), ALU.mult).then_inc(qn_ready, 1)

            def v_context(b):
                dve.wait_ge(ctx_ready, b + 1)
                nc.vector.tensor_tensor(CT, ps[:, 0:P], bmask[:, :], ALU.mult).then_inc(ct_sb, 1)
                dve.wait_ge(ek_ready, b + 1)
                link(nc.vector.reciprocal(ksum[:, 1:2], ksum[:, 0:1]))
                dve.wait_ge(m1_ready, b + 1)
                nc.vector.tensor_scalar_mul(M1, ps[:, HALF:HALF + P], ksum[:, 1:2]).then_inc(m1_sb, 1)

            def v_attend(b):
                dve.wait_ge(att_ready, b + 1)
                t = t2[:, b, :, :].rearrange("p j c -> p (j c)")
                link(nc.vector.scalar_tensor_tensor(t, bank(0, 2), br_c, t, ALU.add, ALU.add))
                layer_norm(t2[:, b, :, :], F, B + 3 * b + 1, n2_ready)
                dve.wait_ge(n2_ready, b + 1)
                layer_norm(F, X2[:, b, :, :], B + 3 * b + 2, x2_ready)

            def v_route(b):
                dve.wait_ge(lg_ready, b + 1)
                link(nc.vector.tensor_tensor(lg[:, :, :], ps[:, 0:J * E].rearrange("p (j e) -> p j e", j=J),
                                             rb[:, :].unsqueeze(1).broadcast_to([P, J, E]), ALU.add))

                def spread(i):
                    return lst2[:, :, i].unsqueeze(2).broadcast_to([P, J, E])

                link(nc.vector.tensor_reduce(lst2[:, :, 0], lg[:, :, :], AX, ALU.max))
                nc.vector.tensor_tensor(lg[:, :, :], lg[:, :, :], spread(0), ALU.subtract).then_inc(lsub_ready, 1)
                dve.wait_ge(lexp_ready, b + 1)
                link(nc.vector.tensor_reduce(lst2[:, :, 1], lg[:, :, :], AX, ALU.add))
                link(nc.vector.reciprocal(lst2[:, :, 2], lst2[:, :, 1]))
                link(nc.vector.tensor_tensor(lg[:, :, :], lg[:, :, :], spread(2), ALU.mult))
                for j in range(J):
                    last = nc.vector.max(top[:, j, :], lg[:, j, :])
                link(last)
                for j in range(J):
                    last = nc.vector.max_index(topi[:, j, :], top[:, j, :], lg[:, j, :])
                link(last)
                nc.vector.tensor_copy(topf[:, :, :], topi[:, :, 0:2])
                link(nc.vector.tensor_tensor(lst2[:, :, 3], top[:, :, 0], top[:, :, 1], ALU.add))
                link(nc.vector.reciprocal(lst2[:, :, 0], lst2[:, :, 3]))
                nc.vector.tensor_tensor(wts[:, b, :, :], top[:, :, 0:2],
                                        lst2[:, :, 0].unsqueeze(2).broadcast_to([P, J, 2]), ALU.mult)
                for w in range(2):
                    last = nc.vector.tensor_tensor(hot[:, w, :, :], iota_e[:, :].unsqueeze(2).broadcast_to([P, E, J]),
                                                   topf[:, :, w].unsqueeze(1).broadcast_to([P, E, J]), ALU.is_equal)
                link(last)
                nc.vector.tensor_tensor(mask[:, :, :], hot[:, 0, :, :], hot[:, 1, :, :], ALU.add).then_inc(mask_ready, 1)
                dve.wait_ge(cum_ready, b + 1)
                link(nc.vector.tensor_copy(tot.rearrange("p e j -> p (e j)"), ps[:, HALF + E * J:HALF + 2 * E * J]))
                link(nc.vector.tensor_tensor_scan(incl.rearrange("p e j -> p (e j)"),
                                                  seg[:, :, :].rearrange("p e j -> p (e j)"),
                                                  tot.rearrange("p e j -> p (e j)"), 0.0, ALU.mult, ALU.add))
                nc.vector.tensor_tensor(slotv, incl, tot, ALU.subtract)
                link(nc.vector.tensor_scalar_add(cnt_i[:, :], incl[:, :, J - 1], float(P - 1)))
                link(nc.vector.tensor_scalar(cnt_i[:, :], cnt_i[:, :], 7, 7, ALU.arith_shift_right, ALU.logical_shift_left))
                link(nc.vector.tensor_copy(cnt[:, 0, :], cnt_i[:, :]))
                link(nc.vector.tensor_tensor_scan(cnt[:, 1, :], ones[:, 0:E], cnt[:, 0, :], 0.0, ALU.mult, ALU.add))
                link(nc.vector.tensor_tensor(cnt[:, 2, :], cnt[:, 1, :], cnt[:, 0, :], ALU.subtract))
                link(nc.vector.tensor_tensor(slotv, slotv,
                                             cnt[:, 2, :].unsqueeze(2).broadcast_to([P, E, J]), ALU.add))
                link(nc.vector.tensor_tensor(slotv, slotv,
                                             ps[:, HALF:HALF + E * J].rearrange("p (e j) -> p e j", e=E), ALU.add))
                for w in range(2):
                    link(nc.vector.tensor_tensor(hot[:, w, :, :], hot[:, w, :, :], slotv, ALU.mult))
                    link(nc.vector.tensor_reduce(slotf[:, w, :], hot[:, w, :, :].rearrange("p e j -> p j e"), AX, ALU.add))
                nc.vector.tensor_copy(slots[:, b, :, :], slotf[:, :, :]).then_inc(slots_ready, 1)
                link(nc.vector.tensor_tensor(cmp, t_iota[:, :, :],
                                             cnt[0:1, 1, :].unsqueeze(1).broadcast_to([1, TILES, E]), ALU.is_ge))
                link(nc.vector.tensor_reduce(tabf[:, :], cmp, AX, ALU.add))
                nc.vector.tensor_scalar_min(tab[0:1, b, :], tabf[:, :], float(E - 1)).then_inc(tab_ready, 1)

            layer1 = [v_tokens, v_key_max, v_query_value, v_query_softmax, v_context, v_attend, v_route]

            def expert_weights():
                dve.wait_ge(o_used, 2 * UNITS)
                dve.wait_ge(ld_b1, 16)
                for e in range(E):
                    if e >= 2:
                        dve.wait_ge(bias_done, e - 1)
                    col = vcol[:, 5 + E + e:6 + E + e]
                    nc.vector.tensor_scalar(H1[:, e % 2, 0:P], ones[:, :], col, None, ALU.mult).then_inc(bias_ready, 1)
                    if e >= 1:
                        dve.wait_ge(bias_done, e)
                        nc.vector.tensor_tensor(bias1[:, e - 1, :], bias1[:, e - 1, :], bank((e - 1) % 2 + 6), ALU.add)
                dve.wait_ge(bias_done, E)
                nc.vector.tensor_tensor(bias1[:, E - 1, :], bias1[:, E - 1, :], bank((E - 1) % 2 + 6), ALU.add)
                for e in range(E):
                    last = nc.vector.tensor_scalar_mul(w1[:, e, :], w1[:, e, :], vcol[:, 5 + e:6 + e])
                last.then_inc(w1_scaled, 1)
                dve.wait_ge(w1_scaled, 1)

            group_norm(0)
            split(0)
            group_norm(1)
            split(1)
            dve.wait_ge(consts_ready, 2)
            for i in range(RING):
                max_slot(0, i)
            for u in range(UNITS):
                for step in range(STEPS):
                    if u + 1 < UNITS:
                        for i in range(2 * step, 2 * step + 2):
                            max_slot(u + 1, i)
                    if step == KT + 1:
                        normalise(u, 0)
                if u + 1 < UNITS:
                    max_slot(u + 1, RING - 1)
                normalise(u, 1)
            dve.wait_ge(ld_rows, 16 * 4)
            for b in range(B):
                for part in layer1:
                    part(b)
            expert_weights()

            def experts(b):
                def x_copy(s, turn):
                    p = parity(b, s)
                    n = TILES * b + s + 2 * turn
                    dve.wait_ge(xT_ready, n + 1)
                    if TILES * b + s >= 2:
                        dve.wait_ge(h_ready, n - 1)
                    nc.vector.tensor_copy(XTT[:, p, :], ps[:, p * P:(p + 1) * P]).then_inc(xT_sb, 1)

                def step(s, turn):
                    n = TILES * b + s + 2 * turn
                    if s == 0:
                        x_copy(0, 0)
                    if is_tile(s):
                        p = parity(b, s)
                        e = dve.value_load(tab[0:1, b, bass.ds(s + 2 * turn, 1)], min_val=0, max_val=E - 1)
                        dve.wait_ge(h_ready, n + 1)
                        if TILES * b + s >= 2:
                            dve.wait_ge(g_ready, n - 1)
                        nc.vector.tensor_tensor(H1[:, p, :], bank(1 + p), bias1[:, e, :], ALU.add).then_inc(h_sb, 1)
                    if is_tile(s + 1):
                        x_copy(s + 1, turn)
                    if is_tile(s - 2):
                        p = parity(b, s - 2)
                        e = dve.value_load(tab[0:1, b, bass.ds(s - 2 + 2 * turn, 1)], min_val=0, max_val=E - 1)
                        dve.wait_ge(y_ready, n - 1)
                        before = earlier(b, s - 2, p)
                        if before:
                            dve.wait_ge(y_out[p], 16 * (before + turn))
                        nc.vector.tensor_tensor(Y[:, p, :], ps[:, (5 + p) * HALF:(5 + p) * HALF + D], bias2[:, e, :],
                                                ALU.add).then_inc(y_sb, 1)

                dve.wait_ge(tab_ready, b + 1)
                expert_steps(dve, b, step)

            dve.wait_ge(ld_b2, 16)
            for b in range(B):
                experts(b)
            for b in range(B):
                dve.wait_ge(gathered[b], 16 * 2 * J)
                for w in range(2):
                    for j in range(J):
                        t = t2[:, b, j, :]
                        last = nc.vector.scalar_tensor_tensor(t, YG[:, 2 * j + w, :], wts[:, b, j, w:w + 1], t, ALU.mult,
                                                              ALU.add)
                    if w == 0:
                        link(last)
                last.then_inc(mix_ready, 1)


_INS = ['x', 'L0_conv_gn_weight', 'L0_conv_gn_bias', 'L0_conv_qkv_weight', 'L0_conv_out_weight', 'L0_conv_out_bias',
        'L1_attn_Wk', 'L1_attn_bk', 'L1_attn_Wq', 'L1_attn_bq', 'L1_attn_Wv', 'L1_attn_bv', 'L1_attn_Wr', 'L1_attn_br',
        'L1_ffn_Wr', 'L1_ffn_br', 'L1_ffn_ln_g', 'L1_ffn_ln_b', 'L1_ffn_W1', 'L1_ffn_b1', 'L1_ffn_W2', 'L1_ffn_b2']
_OUT = ((2, 128, 32, 32), 'float32')


def kernel(**inputs):
    import numpy as _np
    import concourse.bacc as _bacc
    from concourse import mybir as _mybir
    from concourse.bass_utils import run_bass_kernel_spmd as _run

    nc = _bacc.Bacc("TRN2", target_bir_lowering=False, num_devices=1)
    arrays, args = {}, []
    for name in _INS:
        a = _np.ascontiguousarray(inputs[name])
        arrays[f"in_{name}"] = a
        args.append(nc.dram_tensor(f"in_{name}", a.shape, _mybir.dt.from_np(a.dtype), kind="ExternalInput").ap())
    shape, dtype = _OUT
    args.append(nc.dram_tensor("out_0", shape, _mybir.dt.from_np(_np.dtype(dtype)), kind="ExternalOutput").ap())
    build_program(nc, *args)
    r = _run(nc, [arrays], core_ids=[0])
    return r.results[0]["out_0"]
```

```python
import concourse.bass as bass
from concourse import mybir
from contextlib import ExitStack
from math import sqrt


def build_program(nc, x, gn_weight, gn_bias, qkv_weight, out_weight, out_bias, Wk, bk, Wq, bq, Wv, bv, Wr, br,
                  router_w, router_b, ln_g, ln_b, W1, b1, W2, b2, out):
    f32, f32r = mybir.dt.float32, mybir.dt.float32r
    i32, u32 = mybir.dt.int32, mybir.dt.uint32
    ALU, ACT, AX = mybir.AluOpType, mybir.ActivationFunctionType, mybir.AxisListType.X

    B, C, H_, W_ = x.shape
    L = H_ * W_
    P = 128
    J = L // P
    HALF = 512
    HEADS0, HD = 4, 32
    PAIRS = HEADS0 // 2
    UNITS = B * PAIRS
    QT, KT = L // P, L // P
    STEPS = 2 * KT
    SCORE_SCALE = 1.0 / sqrt(C)
    HEADS1, HK = 8, 16
    E, D, HID = W1.shape
    HC = HID // P
    TILES = (2 * L + E * (P - 1)) // P
    EPS = 1e-5
    STORE_LAG = 5
    GROUPS = J // 2
    SPLIT = 3 * HD
    STACK = SPLIT + 2
    QH = QT // 2
    RING = 2 * 2 * QH + 1
    SLOTS = 2 * UNITS * RING

    xs = [nc.dram_tensor(f"expert_in_{b}", (TILES * P, D), f32).ap() for b in range(B)]
    ys = [nc.dram_tensor(f"expert_out_{b}", (TILES * P, D), f32).ap() for b in range(B)]

    ctx = ExitStack()
    with ctx:
        base = nc.sbuf_base
        room = [0]
        ctx.enter_context(nc.sbuf_tensor("slab", [P, 208 * 1024 - 512], mybir.dt.uint8))
        start = (base + 31) // 32 * 32

        def at(name, shape, dt, offset):
            size = 4
            for n in shape[1:]:
                size *= n
            return nc.alloc_sbuf_tensor_at(name, list(shape), dt, offset=start + offset), offset + size

        def sb(name, shape, dt=f32):
            t, end = at(name, shape, dt, room[0])
            room[0] = (end + 31) // 32 * 32
            return t

        def sem(name):
            return ctx.enter_context(nc.semaphore(name))

        w1 = sb("w1", [P, E, HID])
        bias1 = sb("bias1", [P, E, HID])
        w2 = sb("w2", [P, E, HC, D])
        bias2 = sb("bias2", [P, E, D])
        wT = sb("wT", [P, 8, P])
        vcol = sb("vcol", [P, 5 + 2 * E])
        bqv = sb("bqv", [P, 2, P])
        rw = sb("rw", [P, E])
        rb = sb("rb", [P, E])
        ident = sb("ident", [P, P])
        ones = sb("ones", [P, P])
        upper = sb("upper", [P, P])
        gmat = sb("gmat", [P, P])
        bmask = sb("bmask", [P, P])
        iota_e = sb("iota_e", [P, E])
        seg = sb("seg", [P, E, J])
        t_iota = sb("t_iota", [1, TILES, E])
        minus_half = sb("minus_half", [P, J])
        X = sb("X", [P, B, L])
        xn = sb("xn", [P, B, L])
        t2 = sb("t2", [P, B, J, P])
        X2 = sb("X2", [P, B, J, P])
        probs = sb("probs", [P, 3, 2 * HALF])
        vT = sb("vT", [P, B, KT, C])
        attn = sb("attn", [P, B, L])
        wrow = attn[:, 0, :].rearrange("p (j c) -> p j c", j=8)
        gn_row, vrow = attn[0:2, 1, 0:P], attn[0:3 + 2 * E, 1, P:2 * P]
        hl_at = room[0]
        q_hi, q_lo, k_hi, k_lo = ([sb(name, [P, L], f32r), at(name + "1", [P, L], f32r, 4 * L * i)[0]]
                                  for i, name in enumerate(("q_hi", "q_lo", "k_hi", "k_lo")))
        stack_at = room[0]
        Qs = sb("Qs", [P, B, HEADS0, L], f32r)
        Ks = sb("Ks", [P, B, HEADS0, L], f32r)
        QV, o = at("QV", [P, J, 2, P], f32, hl_at)
        QT_sb, o = at("QT_sb", [P, L], f32, o)
        F, o = at("F", [P, J, P], f32, o)
        assert o <= stack_at
        EK, EKT = xn[:, 0, :], xn[:, 1, :].rearrange("p (j k) -> p j k", j=J)
        CT, M1 = xn[:, 0, 0:P], xn[:, 0, P:2 * P]
        tot, incl, slotv = (xn[:, 0, 2 * P + i * E * J:2 * P + (i + 1) * E * J].rearrange("p (e j) -> p e j", e=E)
                            for i in range(3))
        hot = xn[:, 0, 4 * P:4 * P + 2 * E * J].rearrange("p (w e j) -> p w e j", w=2, e=E)
        cmp = xn[0:1, 0, 5 * P:5 * P + TILES * E].rearrange("p (t e) -> p t e", e=E)
        XR, o = at("XR", [P, 2, P], f32, stack_at)
        XTT, o = at("XTT", [P, 2, P], f32, o)
        H1, o = at("H1", [P, 2, HID], f32, o)
        G, o = at("G", [P, 2, HID], f32, o)
        GT, o = at("GT", [P, 2, HC, P], f32, o)
        Y, o = at("Y", [P, 2, D], f32, o)
        YG, o = at("YG", [P, B, 2 * J, D], f32, o)
        OUT, o = at("OUT", [P, B, L], f32, o)
        assert o <= stack_at + 2 * B * HEADS0 * L * 4
        gst = sb("gst", [P, B, 2, 6])
        gmv = sb("gmv", [P, B, 2])
        gtmp = sb("gtmp", [P, B, 4])
        ve = sb("ve", [P, 2 + 3 * B, J])
        rstd = sb("rstd", [P, 2 + 3 * B, J])
        lst = sb("lst", [P, J, 6])
        lmv = sb("lmv", [P, J, 2])
        pm = sb("pm", [P, 2, QH, 2])
        negm = sb("negm", [P, 2, QH])
        mhl = sb("mhl", [P, 2, 2, QH], f32r)
        mrow = sb("mrow", [4 * QH, P], f32r)
        rec = sb("rec", [64, HALF])
        sums = X2[0:64, 1, J // 2:, :].rearrange("p j c -> p (j c)")
        rec16 = sb("rec16", [64, HALF // 32])
        kneg = sb("kneg", [P, 2])
        ksum = sb("ksum", [P, 2])
        qst = sb("qst", [P, J, HEADS1, 3])
        lg = sb("lg", [P, J, E])
        lst2 = sb("lst2", [P, J, 4])
        top = sb("top", [P, J, 8])
        topi = sb("topi", [P, J, 8], u32)
        topf = sb("topf", [P, J, 2])
        wts = sb("wts", [P, B, J, 2])
        mask = sb("mask", [P, E, J])
        cnt_i = sb("cnt_i", [P, E], i32)
        cnt = sb("cnt", [P, 3, E])
        slotf = sb("slotf", [P, 2, J])
        slots = sb("slots", [P, B, 2, J], u32)
        tabf = sb("tabf", [1, TILES])
        tab = sb("tab", [1, B, TILES], i32)
        assert start + room[0] <= nc.sbuf_usable_end

        ps = ctx.enter_context(nc.psum_tensor("ps", [P, 8 * HALF], f32))

        def bank(i, n=1):
            return ps[:, i * HALF:(i + n) * HALF]

        ld_x = [sem(f"ld_x{b}") for b in range(B)]
        ld_wqkv, ld_w, ld_gn, ld_vec, ld_rows = sem("ld_wqkv"), sem("ld_w"), sem("ld_gn"), sem("ld_vec"), sem("ld_rows")
        ld_w1, ld_b1, ld_w2, ld_b2 = sem("ld_w1"), sem("ld_b1"), sem("ld_w2"), sem("ld_b2")
        stack_in = [sem(f"stack_in{u}") for u in range(UNITS)]
        mrow_in = [sem(f"mrow_in{u}_{h}") for u in range(UNITS) for h in range(2)]
        ones_in, xs_zeroed = sem("ones_in"), sem("xs_zeroed")
        scattered = [sem(f"scattered{b}") for b in range(B)]
        gathered = [[sem(f"gathered{b}_{g}") for g in range(J // 2)] for b in range(B)]
        x_in = [sem("x_in_even"), sem("x_in_odd")]
        y_out = [sem("y_out_even"), sem("y_out_odd")]
        stored = sem("stored")
        dve_chain, pool_chain, act_chain = sem("dve_chain"), sem("pool_chain"), sem("act_chain")
        ident_ready, consts_ready = sem("ident_ready"), sem("consts_ready")
        wT_ready, wT_sb = sem("wT_ready"), sem("wT_sb")
        vcol_ready, vcol_sb = sem("vcol_ready"), sem("vcol_sb")
        bias_done, bias_added, w1_scaled = sem("bias_done"), sem("bias_added"), sem("w1_scaled")
        gn_in, gn_out = sem("gn_in"), sem("gn_out")
        var_ready, rstd_ready = sem("var_ready"), sem("rstd_ready")
        xn_ready, resid_ready = sem("xn_ready"), sem("resid_ready")
        qkv_ready, hi_ready, qk_split, v_sb = sem("qkv_ready"), sem("hi_ready"), sem("qk_split"), sem("v_sb")
        slot_ready, slot_used = sem("slot_ready"), sem("slot_used")
        mhl_ready, mrow_ready = sem("mhl_ready"), sem("mrow_ready")
        st_ready, exp_done, pv_done, o_used = sem("st_ready"), sem("exp_done"), sem("pv_done"), sem("o_used")
        proj_ready, t_sb, F_ready = sem("proj_ready"), sem("t_sb"), sem("F_ready")
        keys_ready, kneg_ready, ek_ready = sem("keys_ready"), sem("kneg_ready"), sem("ek_ready")
        qv_ready, qv_sb = sem("qv_ready"), sem("qv_sb")
        ekT_ready, ekT_sb = sem("ekT_ready"), sem("ekT_sb")
        qsub_ready, qexp_ready, qn_ready = sem("qsub_ready"), sem("qexp_ready"), sem("qn_ready")
        ctx_ready, ct_sb, m1_ready, m1_sb = sem("ctx_ready"), sem("ct_sb"), sem("m1_ready"), sem("m1_sb")
        qT_ready, qT_sb, att_ready, n2_ready = sem("qT_ready"), sem("qT_sb"), sem("att_ready"), sem("n2_ready")
        n2T_ready, n2T_sb, lg_ready = sem("n2T_ready"), sem("n2T_sb"), sem("lg_ready")
        lsub_ready, lexp_ready = sem("lsub_ready"), sem("lexp_ready")
        mask_ready, cum_ready, slots_ready, tab_ready = sem("mask_ready"), sem("cum_ready"), sem("slots_ready"), sem("tab_ready")
        x2_ready = sem("x2_ready")
        xT_ready, xT_sb, h_ready, h_sb = sem("xT_ready"), sem("xT_sb"), sem("h_ready"), sem("h_sb")
        g_ready, gT_ready, gT_sb = sem("g_ready"), sem("gT_ready"), sem("gT_sb")
        y_ready, y_sb = sem("y_ready"), sem("y_sb")
        mix_ready, outT_ready, out_sb = sem("mix_ready"), sem("outT_ready"), sem("out_sb")

        def head(u, hd):
            return 2 * (u % PAIRS) + hd

        QV_BANK = ((0, 0), (2, 4))
        GN_BANK = (3, 1)
        LOOP_FROM, STRIDE = 4, 6
        TURNS = (TILES - 5) // STRIDE
        LOOP_TO = LOOP_FROM + STRIDE * TURNS
        LAST = TILES + 2

        order = [(k, i) for k in range(2 * UNITS) for i in range(RING - 1)]
        for k in range(2 * UNITS):
            order.insert(min(RING * (k + 1) + 1, len(order)), (k, "rows"))
        assert len(order) == SLOTS
        place = {slot: g for g, slot in enumerate(order)}

        AHEAD = RING + 6

        def slots_by(s):
            return min(SLOTS, AHEAD + -(-(SLOTS - AHEAD) * s // (2 * STEPS)))

        BIAS_AT = {2 * STEPS + i: (2 * i, 2 * i + 1) for i in range(E // 2)}
        LAYER1_AT = {36: "project", 38: "tokens", 40: "keys", 42: "query_value", 44: "keyT", 46: "queries",
                     47: "context", 49: "queryT", 51: "attend", 54: "norm", 57: "norm2", 58: "tokenT", 60: "logits",
                     62: "route", 63: "counts"}
        BEGIN_LAYER1 = 2 * STEPS + 4
        LAYER1_AT_TILE = {"before": "project tokens keys query_value", 0: "keyT", 1: "queries", 2: "context",
                          3: "queryT", 4: "attend", 5: "norm", 6: "norm2", 7: "tokenT", 8: "logits", 9: "route",
                          10: "counts"}

        def run_parts(parts, where, step, b):
            for name in where.get(step, "").split():
                for part in parts.get(name, []):
                    part(b)

        def parity(b, t):
            return (TILES * b + t) % 2

        def earlier(b, t, p):
            n = TILES * b + t
            return (n + 1 - p) // 2

        def expert_steps(engine, b, step, layer1):
            if b == 0:
                for s in range(LAST):
                    step(s, 0)
                    run_parts(layer1, LAYER1_AT_TILE, s, 1)
                return
            for s in range(LOOP_FROM):
                step(s, 0)
            with engine.Fori(0, TURNS) as turn:
                for s in range(LOOP_FROM, LOOP_FROM + STRIDE):
                    step(s, turn)
            for s in range(LOOP_TO, LAST):
                step(s, 0)

        def is_tile(t):
            return 0 <= t < TILES

        block = ctx.enter_context(nc.Block())

        @block.sync
        def _(sp):
            sp.dma_start(X[:, 0, :], x[0].rearrange("c h w -> c (h w)")).then_inc(ld_x[0], 16)
            for i, v in enumerate((gn_weight, gn_bias)):
                sp.dma_start(gn_row[i:i + 1, :], v.rearrange("(a c) -> a c", a=1)).then_inc(ld_gn, 16)
            sp.dma_start(X[:, 1, :], x[1].rearrange("c h w -> c (h w)")).then_inc(ld_x[1], 16)
            for i, v in enumerate((out_bias, bk, br)):
                sp.dma_start(vrow[i:i + 1, :], v.rearrange("(a c) -> a c", a=1)).then_inc(ld_vec, 16)
            for i, v in enumerate((ln_g, ln_b)):
                sp.dma_start(vrow[3 + i * E:3 + (i + 1) * E, :], v).then_inc(ld_vec, 16)
            sp.dma_start(bqv[:, 0, :], bq.rearrange("(a c) -> a c", a=1).broadcast_to([P, P])).then_inc(ld_rows, 16)
            sp.dma_start(bqv[:, 1, :], bv.rearrange("(a c) -> a c", a=1).broadcast_to([P, P])).then_inc(ld_rows, 16)
            sp.dma_start(rb[:, :], router_b.rearrange("(a c) -> a c", a=1).broadcast_to([P, E])).then_inc(ld_rows, 16)
            sp.dma_start(rw[:, :], router_w).then_inc(ld_rows, 16)
            sp.wait_ge(consts_ready, 1)
            sp.dma_start(Ks[SPLIT:STACK, :, :, :].bitcast(f32).rearrange("s b n (t q) -> s (b n t) q", q=P),
                         ones[:, :]).then_inc(ones_in, 16)

            def stacks(u):
                b = u // PAIRS
                sp.wait_ge(hi_ready, 2 * b + 2)
                sp.wait_ge(qk_split, 2 * b + 2)
                for hd in range(2):
                    n = head(u, hd)
                    rows = slice(n * HD, (n + 1) * HD)
                    for st, parts in ((Qs, (q_hi[b], q_hi[b], q_lo[b])), (Ks, (k_hi[b], k_lo[b], k_hi[b]))):
                        for r, part in enumerate(parts):
                            sp.dma_start(st[r * HD:(r + 1) * HD, b, n, :].bitcast(f32),
                                         part[rows, :].bitcast(f32)).then_inc(stack_in[u], 16)

            def max_rows(u, qh):
                b, k = u // PAIRS, 2 * u + qh
                sp.wait_ge(mrow_ready, k + 1)
                for hd in range(2):
                    dst = Qs[SPLIT:STACK, b, head(u, hd), qh * HALF:(qh + 1) * HALF]
                    sp.dma_start(dst.bitcast(f32).rearrange("s (t q) -> s t q", t=QH),
                                 mrow[hd * 2 * QH:(hd + 1) * 2 * QH, :].bitcast(f32)).then_inc(mrow_in[k], 16)

            stacks(0)
            stacks(1)
            max_rows(0, 0)
            stacks(2)
            stacks(3)
            for u in range(PAIRS, UNITS):
                sp.wait_ge(stack_in[u], 16 * 12)
            sp.dma_start(w1[:, :, :], W1.rearrange("e d h -> d e h")).then_inc(ld_w1, 16)
            max_rows(0, 1)
            sp.dma_start(bias1[:, :, :].rearrange("p e h -> p (e h)"),
                         b1.rearrange("(a e) h -> a (e h)", a=1).broadcast_to([P, E * HID])).then_inc(ld_b1, 16)
            max_rows(1, 0)
            for e in range(E):
                sp.dma_start(w2[:, e, :, :], W2[e].rearrange("(c p) d -> p c d", p=P)).then_inc(ld_w2, 16)
            sp.dma_start(bias2[:, :, :].rearrange("p e h -> p (e h)"),
                         b2.rearrange("(a e) h -> a (e h)", a=1).broadcast_to([P, E * D])).then_inc(ld_b2, 16)
            for k in range(3, 2 * UNITS):
                max_rows(k // 2, k % 2)

            def expert_io(b):
                sp.wait_ge(scattered[b], 16 * 2 * J)

                def step(s, turn):
                    t = s + 2 * turn
                    if is_tile(s):
                        p = parity(b, s)
                        if TILES * b + s >= 2:
                            sp.wait_ge(xT_ready, TILES * b - 1 + t)
                        sp.dma_start(XR[:, p, :], xs[b][bass.ts(t, P), :]).then_inc(x_in[p], 16)
                    if is_tile(s - STORE_LAG):
                        p = parity(b, s - STORE_LAG)
                        sp.wait_ge(y_sb, TILES * b + t - STORE_LAG + 1)
                        sp.dma_start(ys[b][bass.ts(t - STORE_LAG, P), :], Y[:, p, :]).then_inc(y_out[p], 16)

                turns = (TILES - STORE_LAG) // 2
                for s in range(STORE_LAG):
                    step(s, 0)
                with sp.Fori(0, turns) as turn:
                    for s in range(STORE_LAG, STORE_LAG + 2):
                        step(s, turn)
                for s in range(STORE_LAG + 2 * turns, TILES + STORE_LAG):
                    step(s, 0)

            for b in range(B):
                expert_io(b)
            for b in range(B):
                sp.wait_ge(out_sb, GROUPS * (b + 1))
                sp.dma_start(out[b].rearrange("c h w -> c (h w)"), OUT[:, b, :]).then_inc(stored, 16)
            sp.wait_ge(stored, 16 * B)

        @block.gpsimd
        def _(pool):
            chain = [0]

            def link(ins):
                chain[0] += 1
                ins.then_inc(pool_chain, 1)
                pool.wait_ge(pool_chain, chain[0])

            def select(t, pattern, base_, mult, op, fill):
                link(nc.gpsimd.affine_select(out=t, in_=t, compare_op=op, fill=fill, base=base_, pattern=pattern,
                                             channel_multiplier=mult))

            link(nc.gpsimd.memset(ident[:, :], 0.0))
            select(ident[:, :], [[-1, P]], 0, 1, ALU.not_equal, 1.0)
            nc.gpsimd.memset(minus_half[:, :], -0.5).then_inc(ident_ready, 1)

            def blocks(t, value, size):
                link(nc.gpsimd.memset(t[:, :], value))
                v = t[:, :].rearrange("p (g i) -> p g i", i=size)
                select(v, [[-size, P // size], [0, size]], 0, 1, ALU.is_ge, 0.0)
                select(v, [[size, P // size], [0, size]], size - 1, -1, ALU.is_ge, 0.0)

            blocks(gmat, 1.0 / 8, 8)
            nc.gpsimd.memset(ones[:, :], 1.0).then_inc(consts_ready, 1)

            def rsqrt(i):
                n = 1 if i < B else J
                pool.wait_ge(var_ready, i + 1)
                nc.gpsimd.tensor_tensor(rstd[:, i, 0:n], ve[:, i, 0:n], minus_half[:, 0:n], ALU.pow).then_inc(rstd_ready, 1)

            rsqrt(0)
            rsqrt(1)
            pool.wait_ge(vcol_sb, 2)
            for b in range(B):
                pool.wait_ge(xn_ready, b + 1)
                nc.gpsimd.tensor_scalar(X[:, b, :], X[:, b, :], vcol[:, 2:3], None, ALU.add).then_inc(resid_ready, 1)
            blocks(bmask, 1.0, HK)
            link(nc.gpsimd.memset(upper[:, :], 1.0))
            select(upper[:, :], [[1, P]], 0, -1, ALU.is_gt, 0.0)
            nc.gpsimd.iota(iota_e[:, :], [[1, E]], base=0, channel_multiplier=0,
                           allow_small_or_imprecise_dtypes=True)
            nc.gpsimd.iota(t_iota[:, :, :], [[P, TILES], [0, E]], base=0, channel_multiplier=0,
                           allow_small_or_imprecise_dtypes=True)
            link(nc.gpsimd.memset(seg[:, :, :], 1.0))
            nc.gpsimd.memset(seg[:, :, 0:1], 0.0).then_inc(consts_ready, 1)
            per = TILES * D // 2
            zeros = X2[:, :, :, :].rearrange("p b j d -> p (b j d)")[:, 0:per]
            link(nc.gpsimd.memset(zeros, 0.0))
            pool.wait_ge(mhl_ready, 1)
            for b in range(B):
                v = xs[b].rearrange("(p r) d -> p (r d)", p=P)
                for i in range(2):
                    pool.dma_start(v[:, i * per:(i + 1) * per], zeros).then_inc(xs_zeroed, 16)
            pool.wait_ge(xs_zeroed, 16 * 2 * B)

            def scatter(b, between):
                pool.wait_ge(slots_ready, b + 1)
                pool.wait_ge(x2_ready, b + 1)
                for j in range(J):
                    between(j)
                    for w in range(2):
                        pool.indirect_dma_start(xs[b][:, :], bass.IndirectOffsetOnAxis(ap=slots[:, b, w, j:j + 1], axis=0),
                                                X2[:, b, j, :], None).then_inc(scattered[b], 16)

            def gather(b):
                for p in range(2):
                    pool.wait_ge(y_out[p], 16 * earlier(b, TILES, p))
                for j in range(J):
                    for w in range(2):
                        pool.indirect_dma_start(YG[:, b, 2 * j + w, :], None, ys[b][:, :],
                                                bass.IndirectOffsetOnAxis(ap=slots[:, b, w, j:j + 1], axis=0)
                                                ).then_inc(gathered[b][j // 2], 16)

            rsqrt(B)
            pool.wait_ge(bias_done, E)
            for e in range(E):
                last = nc.gpsimd.tensor_scalar(w1[:, e, :], w1[:, e, :], vcol[:, 5 + e:6 + e], None, ALU.mult)
            last.then_inc(w1_scaled, 1)
            pool.wait_ge(w1_scaled, 1)
            rsqrt(B + 1)
            rsqrt(B + 2)
            scatter(0, lambda j: rsqrt(B + 3) if j == J // 2 else None)
            rsqrt(B + 4)
            rsqrt(B + 5)
            scatter(1, lambda j: None)
            for b in range(B):
                gather(b)

        @block.scalar
        def _(act):
            for n in range(HEADS0):
                src = qkv_weight[n * SPLIT:(n + 1) * SPLIT, :].rearrange("(s i) c -> i s c", s=3)
                act.dma_start(wrow[n * HD:(n + 1) * HD, 0:3, :], src).then_inc(ld_wqkv, 16)
            for n, w in enumerate((out_weight, Wq, Wv, Wk, Wr)):
                act.dma_start(wrow[:, 3 + n, :], w).then_inc(ld_w, 16)
            act.wait_ge(wT_ready, 1)
            nc.scalar.activation(wT[:, 0:3, :], ps[:, 0:3 * P].rearrange("p (j c) -> p j c", j=3),
                                 ACT.Copy).then_inc(wT_sb, 1)

            def split(b):
                act.wait_ge(qkv_ready, 3 * b + 1)
                nc.scalar.activation(q_hi[b][:, :], bank(4, 2), ACT.Copy, scale=SCORE_SCALE).then_inc(hi_ready, 1)
                act.wait_ge(qkv_ready, 3 * b + 2)
                nc.scalar.activation(k_hi[b][:, :], bank(6, 2), ACT.Copy).then_inc(hi_ready, 1)
                act.wait_ge(qkv_ready, 3 * b + 3)
                nc.scalar.activation(vT[:, b, :, :].rearrange("p t c -> p (t c)"), bank(2, 2), ACT.Copy).then_inc(v_sb, 1)

            def exps(u, step):
                s = u * STEPS + step
                act.wait_ge(st_ready, s + 1)
                if s >= 3:
                    act.wait_ge(pv_done, s - 2)
                nc.scalar.activation(probs[:, s % 3, :], bank(2 + 2 * (s % 2), 2), ACT.Exp).then_inc(exp_done, 1)

            def a_tokens(b):
                act.wait_ge(proj_ready, b + 1)
                nc.scalar.activation(t2[:, b, :, :].rearrange("p j c -> p (j c)"), bank(2 * b, 2),
                                     ACT.Copy).then_inc(t_sb, 1)

            def a_key_exp(b):
                act.wait_ge(kneg_ready, b + 1)
                nc.scalar.activation(EK, bank(0, 2), ACT.Exp, bias=kneg[:, 1:2],
                                     accum_out=ksum[:, 0:1]).then_inc(ek_ready, 1)

            def a_keyT(b):
                act.wait_ge(ekT_ready, b + 1)
                nc.scalar.activation(xn[:, 1, :], bank(0, 2), ACT.Copy).then_inc(ekT_sb, 1)

            def a_query_exp(b):
                act.wait_ge(qsub_ready, b + 1)
                q = QV[:, :, 0, :]
                nc.scalar.activation(q, q, ACT.Exp).then_inc(qexp_ready, 1)

            def a_queryT(b):
                act.wait_ge(qT_ready, b + 1)
                nc.scalar.activation(QT_sb[:, :], bank(0, 2), ACT.Copy).then_inc(qT_sb, 1)

            def a_tokenT(b):
                act.wait_ge(n2T_ready, b + 1)
                nc.scalar.activation(QT_sb[:, :], bank(0, 2), ACT.Copy).then_inc(n2T_sb, 1)

            def a_route(b):
                act.wait_ge(lsub_ready, b + 1)
                nc.scalar.activation(lg[:, :, :], lg[:, :, :], ACT.Exp).then_inc(lexp_ready, 1)

            layer1 = {"project": [a_tokens], "keys": [a_key_exp], "keyT": [a_keyT, a_query_exp], "queryT": [a_queryT],
                      "tokenT": [a_tokenT], "logits": [a_route]}

            split(0)
            act.wait_ge(wT_ready, 2)
            nc.scalar.activation(wT[:, 3:8, :], ps[:, 0:5 * P].rearrange("p (j c) -> p j c", j=5),
                                 ACT.Copy).then_inc(wT_sb, 1)
            nc.scalar.activation(vcol[:, 2:], ps[:, 5 * P:5 * P + 3 + 2 * E], ACT.Copy).then_inc(vcol_sb, 1)
            split(1)
            for s in range(UNITS * STEPS):
                exps(s // STEPS, s % STEPS)
                run_parts(layer1, LAYER1_AT, s, 0)
            run_parts(layer1, LAYER1_AT_TILE, "before", 1)

            def experts(b):
                def step(s, turn):
                    n = TILES * b + s + STRIDE * turn
                    if is_tile(s):
                        p = parity(b, s)
                        act.wait_ge(h_sb, n + 1)
                        if TILES * b + s >= 2:
                            act.wait_ge(gT_ready, n - 1)
                        nc.scalar.activation(G[:, p, :], H1[:, p, :], ACT.Gelu).then_inc(g_ready, 1)
                    if is_tile(s - 1):
                        p = parity(b, s - 1)
                        act.wait_ge(gT_ready, n)
                        if TILES * b + s >= 3:
                            act.wait_ge(y_ready, n - 2)
                        nc.scalar.activation(GT[:, p, :, :].rearrange("p c t -> p (c t)"), bank(4 + p),
                                             ACT.Copy).then_inc(gT_sb, 1)

                expert_steps(act, b, step, layer1)

            for b in range(B):
                experts(b)
            for b in range(B):
                v = OUT[:, b, :].rearrange("c (d j) -> c d j", j=J)
                for g in range(GROUPS):
                    k = GROUPS * b + g
                    act.wait_ge(outT_ready, k + 1)
                    nc.scalar.activation(v[:, :, 2 * g:2 * g + 2],
                                         bank(k % 2)[:, 0:2 * P].rearrange("c (j d) -> c d j", j=2),
                                         ACT.Copy).then_inc(out_sb, 1)

        @block.tensor
        def _(pe):
            pe.wait_ge(ident_ready, 1)
            pe.wait_ge(ld_gn, 16 * 2)
            nc.tensor.transpose(ps[:, 2 * HALF:2 * HALF + 2], gn_row, ident[0:2, 0:2]).then_inc(vcol_ready, 1)
            pe.wait_ge(ld_wqkv, 16 * HEADS0)
            for j in range(3):
                last = nc.tensor.transpose(ps[:, j * P:(j + 1) * P], wrow[:, j, :], ident[:, :])
            last.then_inc(wT_ready, 1)

            def weight_transposes():
                pe.wait_ge(ld_w, 16 * 5)
                pe.wait_ge(ld_vec, 16 * 5)
                pe.wait_ge(var_ready, B)
                for j in range(5):
                    nc.tensor.transpose(ps[:, j * P:(j + 1) * P], wrow[:, 3 + j, :], ident[:, :])
                n = 3 + 2 * E
                nc.tensor.transpose(ps[:, 5 * P:5 * P + n], vrow, ident[0:n, 0:n]).then_inc(wT_ready, 1)

            def group_stats(b):
                for i in range(2):
                    pe.wait_ge(gn_in, 2 * b + i + 1)
                    if not (b or i):
                        pe.wait_ge(consts_ready, 1)
                    src = gmv[:, b, 0:1] if i == 0 else gtmp[:, b, 1:2]
                    nc.tensor.matmul(bank(GN_BANK[b])[:, i:i + 1], gmat[:, :], src,
                                     start=True, stop=True).then_inc(gn_out, 1)

            def queries_keys(b):
                pe.wait_ge(xn_ready, b + 1)
                if b == 0:
                    pe.wait_ge(wT_sb, 1)
                for i, at_ in ((0, 4), (1, 6)):
                    if b:
                        pe.wait_ge(qk_split, i + 1)
                    for h in range(2):
                        last = nc.tensor.matmul(bank(at_ + h), wT[:, i, :], xn[:, b, h * HALF:(h + 1) * HALF],
                                                start=True, stop=True)
                    last.then_inc(qkv_ready, 1)

            def values_of(b):
                if b == 0:
                    pe.wait_ge(vcol_sb, 1)
                else:
                    pe.wait_ge(v_sb, b)
                for t in range(KT):
                    last = nc.tensor.matmul(ps[:, 2 * HALF + t * P:2 * HALF + (t + 1) * P],
                                            xn[:, b, t * P:(t + 1) * P], wT[:, 2, :], start=True, stop=True)
                last.then_inc(qkv_ready, 1)

            def max_slot(g):
                k, i = order[g]
                u, qh = k // 2, k % 2
                b = u // PAIRS
                if i == 0 and qh == 0:
                    pe.wait_ge(stack_in[u], 16 * 12)
                if g >= 2:
                    pe.wait_ge(slot_used, g - 1)
                elif g == 0:
                    pe.wait_ge(wT_sb, 2)
                    pe.wait_ge(vcol_sb, 2)
                if i != "rows":
                    hd, t, h = i // (2 * QH), QH * qh + (i // 2) % QH, i % 2
                    n = head(u, hd)
                    last = nc.tensor.matmul(bank(g % 2), Qs[0:SPLIT, b, n, t * P:(t + 1) * P],
                                            Ks[0:SPLIT, b, n, h * HALF:(h + 1) * HALF], start=True, stop=True)
                else:
                    pe.wait_ge(mhl_ready, k + 1)
                    last = nc.tensor.transpose(ps[0:4 * QH, (g % 2) * HALF:(g % 2) * HALF + P],
                                               mhl[:, :, :, :].bitcast(f32).rearrange("p h s t -> p (h s t)"), ident[:, :])
                last.then_inc(slot_ready, 1)

            def scores(u, step):
                s = u * STEPS + step
                b, qh, kt = u // PAIRS, step // KT, step % KT
                if kt == 0:
                    pe.wait_ge(mrow_in[2 * u + qh], 16 * 2)
                if s >= 2:
                    pe.wait_ge(exp_done, s - 1)
                else:
                    pe.wait_ge(v_sb, B)
                    pe.wait_ge(qk_split, 2 * B)
                    pe.wait_ge(ones_in, 16)
                for hd in range(2):
                    n = head(u, hd)
                    last = nc.tensor.matmul(bank(2 + 2 * (s % 2) + hd), Ks[0:STACK, b, n, kt * P:(kt + 1) * P],
                                            Qs[0:STACK, b, n, qh * HALF:(qh + 1) * HALF], start=True, stop=True)
                last.then_inc(st_ready, 1)

            def values(u, step, hd):
                s = u * STEPS + step
                b, qh, kt = u // PAIRS, step // KT, step % KT
                o = 2 * u + qh
                if hd == 0:
                    pe.wait_ge(exp_done, s + 1)
                    if kt == 0 and o >= 2:
                        pe.wait_ge(o_used, o - 1)
                n = head(u, hd)
                for i, w in ((hd, vT[:, b, kt, n * HD:(n + 1) * HD]), (2 + hd, ones[:, 0:HD])):
                    last = nc.tensor.matmul(bank(6 + o % 2)[i * HD:(i + 1) * HD, :], w,
                                            probs[:, s % 3, hd * HALF:(hd + 1) * HALF],
                                            start=kt == 0, stop=kt == KT - 1)
                if hd:
                    last.then_inc(pv_done, 1)

            def t_project(b):
                pe.wait_ge(o_used, 4 * b + 4)
                pe.wait_ge(resid_ready, b + 1)
                if b == 0:
                    pe.wait_ge(bias_added, E)
                for j in range(J):
                    o = bank(2 * b, 2)[:, j * P:(j + 1) * P]
                    nc.tensor.matmul(o, attn[:, b, j::J], wT[:, 3, :], start=True, stop=False)
                    last = nc.tensor.matmul(o, X[:, b, j::J], ident[:, :], start=False, stop=True)
                last.then_inc(proj_ready, 1)

            def t_keys(b):
                pe.wait_ge(F_ready, b + 1)
                if b:
                    pe.wait_ge(slots_ready, b)
                for h in range(2):
                    last = nc.tensor.matmul(bank(h), wT[:, 6, :], F[:, 4 * h:4 * h + 4, :].rearrange("d j c -> d (j c)"),
                                            start=True, stop=True)
                last.then_inc(keys_ready, 1)

            def t_query_value(b):
                if b == 0:
                    pe.wait_ge(ek_ready, b + 1)
                for h in range(2):
                    if h and b == 0:
                        pe.wait_ge(qv_sb, 2 * b + h)
                    for i in range(J // 2):
                        last = nc.tensor.matmul(bank(QV_BANK[b][h], 2)[:, i * 2 * P:(i + 1) * 2 * P], F[:, 4 * h + i, :],
                                                wT[:, 4:6, :].rearrange("d w k -> d (w k)"), start=True, stop=True)
                    last.then_inc(qv_ready, 1)

            def t_keyT(b):
                pe.wait_ge(ek_ready, b + 1)
                pe.wait_ge(qv_sb, 2 * b + 2)
                for j in range(J):
                    last = nc.tensor.transpose(ps[:, j * P:(j + 1) * P], EK[:, j * P:(j + 1) * P], ident[:, :])
                last.then_inc(ekT_ready, 1)

            def t_context(b):
                pe.wait_ge(ekT_sb, b + 1)
                for j in range(J):
                    last = nc.tensor.matmul(ps[:, 0:P], QV[:, j, 1, :], EKT[:, j, :], start=j == 0, stop=j == J - 1)
                last.then_inc(ctx_ready, 1)
                pe.wait_ge(ct_sb, b + 1)
                nc.tensor.matmul(ps[:, HALF:HALF + P], CT, wT[:, 7, :], start=True, stop=True).then_inc(m1_ready, 1)

            def t_queryT(b):
                pe.wait_ge(qn_ready, b + 1)
                pe.wait_ge(m1_sb, b + 1)
                for j in range(J):
                    last = nc.tensor.transpose(ps[:, j * P:(j + 1) * P], QV[:, j, 0, :], ident[:, :])
                last.then_inc(qT_ready, 1)

            def t_attend(b):
                pe.wait_ge(qT_sb, b + 1)
                for h in range(2):
                    last = nc.tensor.matmul(bank(h), M1, QT_sb[:, h * HALF:(h + 1) * HALF], start=True, stop=True)
                last.then_inc(att_ready, 1)

            def t_tokenT(b):
                pe.wait_ge(n2_ready, b + 1)
                for j in range(J):
                    last = nc.tensor.transpose(ps[:, j * P:(j + 1) * P], F[:, j, :], ident[:, :])
                last.then_inc(n2T_ready, 1)

            def t_logits(b):
                pe.wait_ge(n2T_sb, b + 1)
                for j in range(J):
                    last = nc.tensor.matmul(ps[:, j * E:(j + 1) * E], QT_sb[:, j * P:(j + 1) * P], rw[:, :],
                                            start=True, stop=True)
                last.then_inc(lg_ready, 1)

            def t_counts(b):
                pe.wait_ge(mask_ready, b + 1)
                m = mask[:, :, :].rearrange("p e j -> p (e j)")
                nc.tensor.matmul(ps[:, HALF:HALF + E * J], upper[:, :], m, start=True, stop=True)
                nc.tensor.matmul(ps[:, HALF + E * J:HALF + 2 * E * J], ones[:, :], m, start=True,
                                 stop=True).then_inc(cum_ready, 1)

            layer1 = {"project": [t_project], "keys": [t_keys], "query_value": [t_query_value], "keyT": [t_keyT],
                      "context": [t_context], "queryT": [t_queryT], "attend": [t_attend], "tokenT": [t_tokenT],
                      "logits": [t_logits], "counts": [t_counts]}

            def expert_bias(e):
                if e == 0:
                    pe.wait_ge(ld_w1, 16)
                    pe.wait_ge(slot_used, SLOTS)
                if e >= 2:
                    pe.wait_ge(bias_added, e - 1)
                nc.tensor.matmul(bank(e % 2), vcol[:, 5 + E + e:6 + E + e].broadcast_to([P, P]), w1[:, e, :], start=True,
                                 stop=True).then_inc(bias_done, 1)

            group_stats(0)
            queries_keys(0)
            group_stats(1)
            values_of(0)
            weight_transposes()
            queries_keys(1)
            values_of(1)
            for g in range(slots_by(0)):
                max_slot(g)
            scores(0, 0)
            for s in range(UNITS * STEPS):
                if s + 1 < UNITS * STEPS:
                    scores((s + 1) // STEPS, (s + 1) % STEPS)
                new = range(slots_by(s), slots_by(s + 1))
                third = len(new) // 3
                for g in new[:third]:
                    max_slot(g)
                for e in BIAS_AT.get(s, ()):
                    expert_bias(e)
                if s == BEGIN_LAYER1:
                    pe.wait_ge(consts_ready, 2)
                    pe.wait_ge(ld_rows, 16 * 4)
                run_parts(layer1, LAYER1_AT, s, 0)
                values(s // STEPS, s % STEPS, 0)
                for g in new[third:2 * third]:
                    max_slot(g)
                values(s // STEPS, s % STEPS, 1)
                for g in new[2 * third:]:
                    max_slot(g)
            run_parts(layer1, LAYER1_AT_TILE, "before", 1)

            def experts(b):
                def x_transpose(s, turn):
                    p = parity(b, s)
                    n = TILES * b + s + STRIDE * turn
                    pe.wait_ge(x_in[p], 16 * (earlier(b, s, p) + 1 + STRIDE // 2 * turn))
                    if b == 0 and s == 0:
                        pe.wait_ge(o_used, 2 * UNITS)
                    if s >= 4:
                        pe.wait_ge(y_sb, n - 3)
                    elif b and s < 2:
                        pe.wait_ge(y_sb, n - 1)
                    nc.tensor.transpose(bank(6 + p)[:, P:2 * P], XR[:, p, :], ident[:, :]).then_inc(xT_ready, 1)

                expert_of = {}

                def load_expert(s, turn):
                    key = (s, isinstance(turn, int))
                    if key not in expert_of:
                        expert_of[key] = pe.value_load(tab[0:1, b, bass.ds(s + STRIDE * turn, 1)], min_val=0,
                                                        max_val=E - 1)
                    return expert_of[key]

                def step(s, turn):
                    n = TILES * b + s + STRIDE * turn
                    if s == 0:
                        x_transpose(0, 0)
                    if is_tile(s):
                        p = parity(b, s)
                        e = load_expert(s, turn)
                        pe.wait_ge(xT_sb, n + 1)
                        nc.tensor.matmul(bank(2 + p), XTT[:, p, :], w1[:, e, :], start=True, stop=True).then_inc(h_ready, 1)
                    if is_tile(s - 1):
                        p = parity(b, s - 1)
                        pe.wait_ge(g_ready, n)
                        for c in range(HC):
                            last = nc.tensor.transpose(bank(4 + p)[:, c * P:(c + 1) * P], G[:, p, c * P:(c + 1) * P],
                                                       ident[:, :])
                        last.then_inc(gT_ready, 1)
                    if is_tile(s + 1):
                        x_transpose(s + 1, turn)
                    if is_tile(s - 2):
                        p = parity(b, s - 2)
                        e = load_expert(s - 2, turn)
                        pe.wait_ge(gT_sb, n - 1)
                        if s >= TILES:
                            pe.wait_ge(y_sb, n - 3)
                        for c in range(HC):
                            last = nc.tensor.matmul(bank(6 + p)[:, 0:D], GT[:, p, c, :], w2[:, e, c, :], start=c == 0,
                                                    stop=c == HC - 1)
                        last.then_inc(y_ready, 1)

                if b == 0:
                    pe.wait_ge(w1_scaled, 1)
                    pe.wait_ge(ld_w2, 16 * E)
                pe.wait_ge(tab_ready, b + 1)
                expert_steps(pe, b, step, layer1)

            for b in range(B):
                experts(b)
            pe.wait_ge(slots_ready, B)
            for b in range(B):
                for g in range(GROUPS):
                    k = GROUPS * b + g
                    pe.wait_ge(mix_ready, k + 1)
                    if k >= 2:
                        pe.wait_ge(out_sb, k - 1)
                    for j in range(2):
                        last = nc.tensor.transpose(bank(k % 2)[:, j * P:(j + 1) * P], t2[:, b, 2 * g + j, :], ident[:, :])
                    last.then_inc(outT_ready, 1)

        @block.vector
        def _(dve):
            chain = [0]

            def link(ins):
                chain[0] += 1
                ins.then_inc(dve_chain, 1)
                dve.wait_ge(dve_chain, chain[0])

            dve.wait_ge(vcol_ready, 1)
            nc.vector.tensor_copy(vcol[:, 0:2], ps[:, 2 * HALF:2 * HALF + 2]).then_inc(vcol_sb, 1)
            dve.wait_ge(vcol_sb, 1)
            gn_w, gn_b, bk_c, br_c = (vcol[:, i:i + 1] for i in (0, 1, 3, 4))

            def group_norm(b):
                dve.wait_ge(ld_x[b], 16)
                for h in range(2):
                    last = nc.vector.bn_stats(gst[:, b, h, :], X[:, b, h * HALF:(h + 1) * HALF])
                link(last)
                nc.vector.bn_aggr(gmv[:, b, :], gst[:, b, :, :]).then_inc(gn_in, 1)
                dve.wait_ge(gn_out, 2 * b + 1)
                gm = gtmp[:, b, 2:3]
                link(nc.vector.tensor_copy(gm, bank(GN_BANK[b])[:, 0:1]))
                d = gtmp[:, b, 0:1]
                link(nc.vector.tensor_tensor(d, gmv[:, b, 0:1], gm, ALU.subtract))
                nc.vector.scalar_tensor_tensor(gtmp[:, b, 1:2], d, d, gmv[:, b, 1:2], ALU.mult, ALU.add).then_inc(gn_in, 1)
                dve.wait_ge(gn_out, 2 * b + 2)
                nc.vector.tensor_scalar_add(ve[:, b, 0:1], bank(GN_BANK[b])[:, 1:2], EPS).then_inc(var_ready, 1)
                dve.wait_ge(rstd_ready, b + 1)
                sc = gtmp[:, b, 0:1]
                link(nc.vector.tensor_tensor(sc, rstd[:, b, 0:1], gn_w, ALU.mult))
                link(nc.vector.scalar_tensor_tensor(gtmp[:, b, 3:4], gm, sc, gn_b, ALU.mult, ALU.subtract))
                nc.vector.tensor_scalar(xn[:, b, :], X[:, b, :], sc, gtmp[:, b, 3:4], ALU.mult,
                                        ALU.subtract).then_inc(xn_ready, 1)

            def split(b):
                dve.wait_ge(hi_ready, 2 * b + 1)
                nc.vector.scalar_tensor_tensor(q_lo[b][:, :], bank(4, 2), SCORE_SCALE, q_hi[b][:, :].bitcast(f32), ALU.mult,
                                               ALU.subtract).then_inc(qk_split, 1)
                dve.wait_ge(hi_ready, 2 * b + 2)
                nc.vector.tensor_tensor(k_lo[b][:, :], bank(6, 2), k_hi[b][:, :].bitcast(f32), ALU.subtract).then_inc(qk_split, 1)

            def max_slot(g):
                k, i = order[g]
                if i != "rows":
                    hd, t, h = i // (2 * QH), (i // 2) % QH, i % 2
                    dve.wait_ge(slot_ready, g + 1)
                    nc.vector.tensor_reduce(pm[:, hd, t, h:h + 1], bank(g % 2), AX, ALU.max).then_inc(slot_used, 1)
                    if i == RING - 2:
                        dve.wait_ge(slot_used, g + 1)
                        link(nc.vector.tensor_reduce(negm[:, :, :], pm[:, :, :, :], AX, ALU.max, negate=True))
                        if k:
                            dve.wait_ge(slot_ready, place[k - 1, "rows"] + 1)
                        link(nc.vector.tensor_copy(mhl[:, :, 0, :], negm[:, :, :]))
                        nc.vector.tensor_tensor(mhl[:, :, 1, :], negm[:, :, :], mhl[:, :, 0, :].bitcast(f32),
                                                ALU.subtract).then_inc(mhl_ready, 1)
                    return
                dve.wait_ge(slot_ready, g + 1)
                if k:
                    dve.wait_ge(mrow_in[k - 1], 16 * 2)
                nc.vector.tensor_copy(mrow[:, :], ps[0:4 * QH, (g % 2) * HALF:(g % 2) * HALF + P]).then_inc(mrow_ready, 1)
                dve.wait_ge(mrow_ready, k + 1)
                dve.sem_inc(slot_used, 1)

            def normalise(u, qh):
                o = 2 * u + qh
                b, pair = u // PAIRS, u % PAIRS
                dve.wait_ge(pv_done, u * STEPS + (qh + 1) * KT)
                if o:
                    dve.wait_ge(o_used, o)
                link(nc.vector.transpose(sums[:, :], bank(6 + o % 2)[64:128, :]))
                link(nc.vector.reciprocal(rec16[:, :], sums[:, :].rearrange("p (k c) -> p k c", c=32)[:, :, 0]))
                link(nc.vector.transpose(rec[:, :].rearrange("p (k c) -> p k c", c=32),
                                         rec16[:, :].unsqueeze(2).broadcast_to([64, HALF // 32, 32])))
                nc.vector.tensor_tensor(attn[64 * pair:64 * pair + 64, b, qh * HALF:(qh + 1) * HALF],
                                        bank(6 + o % 2)[0:64, :], rec[:, :], ALU.mult).then_inc(o_used, 1)

            def norm_stats(src, i):
                for j in range(J):
                    last = nc.vector.bn_stats(lst[:, j, :], src[:, j, :])
                link(last)
                for j in range(J):
                    last = nc.vector.bn_aggr(lmv[:, j, :], lst[:, j, :])
                link(last)
                nc.vector.tensor_scalar_add(ve[:, i, :], lmv[:, :, 1], EPS).then_inc(var_ready, 1)

            def norm_apply(src, dst, i, done):
                dve.wait_ge(rstd_ready, i + 1)
                for j in range(J):
                    last = nc.vector.tensor_scalar(dst[:, j, :], src[:, j, :], lmv[:, j, 0:1], rstd[:, i, j:j + 1],
                                                   ALU.subtract, ALU.mult)
                last.then_inc(done, 1)

            def v_project(b):
                dve.wait_ge(t_sb, b + 1)
                norm_stats(t2[:, b, :, :], B + 3 * b)

            def v_tokens(b):
                norm_apply(t2[:, b, :, :], F, B + 3 * b, F_ready)

            def v_key_max(b):
                dve.wait_ge(keys_ready, b + 1)
                link(nc.vector.tensor_reduce(kneg[:, 0:1], bank(0, 2), AX, ALU.max, negate=True))
                nc.vector.tensor_scalar(kneg[:, 1:2], kneg[:, 0:1], bk_c, bk_c, ALU.subtract, ALU.add).then_inc(kneg_ready, 1)

            def v_query_value(b):
                for h in range(2):
                    dve.wait_ge(qv_ready, 2 * b + h + 1)
                    nc.vector.tensor_tensor(QV[:, 4 * h:4 * h + 4, :, :].rearrange("p j w k -> p j (w k)"),
                                            bank(QV_BANK[b][h], 2).rearrange("p (j k) -> p j k", j=4),
                                            bqv[:, :, :].rearrange("p w k -> p (w k)").unsqueeze(1).broadcast_to([P, 4, 2 * P]),
                                            ALU.add).then_inc(qv_sb, 1)

            def spread_query(i):
                return qst[:, :, :, i].unsqueeze(3).broadcast_to([P, J, HEADS1, HK])

            def v_query_max(b):
                dve.wait_ge(qv_sb, 2 * b + 2)
                q = QV[:, :, 0, :].rearrange("p j (h k) -> p j h k", k=HK)

                link(nc.vector.tensor_reduce(qst[:, :, :, 0], q, AX, ALU.max))
                nc.vector.tensor_tensor(q, q, spread_query(0), ALU.subtract).then_inc(qsub_ready, 1)

            def v_queries(b):
                dve.wait_ge(qexp_ready, b + 1)
                q = QV[:, :, 0, :].rearrange("p j (h k) -> p j h k", k=HK)
                link(nc.vector.tensor_reduce(qst[:, :, :, 1], q, AX, ALU.add))
                link(nc.vector.reciprocal(qst[:, :, :, 2], qst[:, :, :, 1]))
                nc.vector.tensor_tensor(q, q, spread_query(2), ALU.mult).then_inc(qn_ready, 1)

            def v_context(b):
                dve.wait_ge(ctx_ready, b + 1)
                nc.vector.tensor_tensor(CT, ps[:, 0:P], bmask[:, :], ALU.mult).then_inc(ct_sb, 1)
                dve.wait_ge(ek_ready, b + 1)
                link(nc.vector.reciprocal(ksum[:, 1:2], ksum[:, 0:1]))
                dve.wait_ge(m1_ready, b + 1)
                nc.vector.tensor_scalar_mul(M1, ps[:, HALF:HALF + P], ksum[:, 1:2]).then_inc(m1_sb, 1)

            def v_attend(b):
                dve.wait_ge(att_ready, b + 1)
                t = t2[:, b, :, :].rearrange("p j c -> p (j c)")
                link(nc.vector.scalar_tensor_tensor(t, bank(0, 2), br_c, t, ALU.add, ALU.add))
                norm_stats(t2[:, b, :, :], B + 3 * b + 1)

            def v_norm(b):
                norm_apply(t2[:, b, :, :], F, B + 3 * b + 1, n2_ready)
                dve.wait_ge(n2_ready, b + 1)
                norm_stats(F, B + 3 * b + 2)

            def v_norm2(b):
                norm_apply(F, X2[:, b, :, :], B + 3 * b + 2, x2_ready)

            def spread_gate(i):
                return lst2[:, :, i].unsqueeze(2).broadcast_to([P, J, E])

            def v_gates(b):
                dve.wait_ge(lg_ready, b + 1)
                link(nc.vector.tensor_tensor(lg[:, :, :], ps[:, 0:J * E].rearrange("p (j e) -> p j e", j=J),
                                             rb[:, :].unsqueeze(1).broadcast_to([P, J, E]), ALU.add))

                link(nc.vector.tensor_reduce(lst2[:, :, 0], lg[:, :, :], AX, ALU.max))
                nc.vector.tensor_tensor(lg[:, :, :], lg[:, :, :], spread_gate(0), ALU.subtract).then_inc(lsub_ready, 1)

            def v_route(b):
                dve.wait_ge(lexp_ready, b + 1)
                link(nc.vector.tensor_reduce(lst2[:, :, 1], lg[:, :, :], AX, ALU.add))
                link(nc.vector.reciprocal(lst2[:, :, 2], lst2[:, :, 1]))
                link(nc.vector.tensor_tensor(lg[:, :, :], lg[:, :, :], spread_gate(2), ALU.mult))
                for j in range(J):
                    last = nc.vector.max(top[:, j, :], lg[:, j, :])
                link(last)
                for j in range(J):
                    last = nc.vector.max_index(topi[:, j, :], top[:, j, :], lg[:, j, :])
                link(last)
                nc.vector.tensor_copy(topf[:, :, :], topi[:, :, 0:2])
                link(nc.vector.tensor_tensor(lst2[:, :, 3], top[:, :, 0], top[:, :, 1], ALU.add))
                link(nc.vector.reciprocal(lst2[:, :, 0], lst2[:, :, 3]))
                nc.vector.tensor_tensor(wts[:, b, :, :], top[:, :, 0:2],
                                        lst2[:, :, 0].unsqueeze(2).broadcast_to([P, J, 2]), ALU.mult)
                for w in range(2):
                    last = nc.vector.tensor_tensor(hot[:, w, :, :], iota_e[:, :].unsqueeze(2).broadcast_to([P, E, J]),
                                                   topf[:, :, w].unsqueeze(1).broadcast_to([P, E, J]), ALU.is_equal)
                link(last)
                nc.vector.tensor_tensor(mask[:, :, :], hot[:, 0, :, :], hot[:, 1, :, :], ALU.add).then_inc(mask_ready, 1)

            def v_slots(b):
                dve.wait_ge(cum_ready, b + 1)
                link(nc.vector.tensor_copy(tot.rearrange("p e j -> p (e j)"), ps[:, HALF + E * J:HALF + 2 * E * J]))
                link(nc.vector.tensor_tensor_scan(incl.rearrange("p e j -> p (e j)"),
                                                  seg[:, :, :].rearrange("p e j -> p (e j)"),
                                                  tot.rearrange("p e j -> p (e j)"), 0.0, ALU.mult, ALU.add))
                nc.vector.tensor_tensor(slotv, incl, tot, ALU.subtract)
                link(nc.vector.tensor_scalar_add(cnt_i[:, :], incl[:, :, J - 1], float(P - 1)))
                link(nc.vector.tensor_scalar(cnt_i[:, :], cnt_i[:, :], 7, 7, ALU.arith_shift_right, ALU.logical_shift_left))
                link(nc.vector.tensor_copy(cnt[:, 0, :], cnt_i[:, :]))
                link(nc.vector.tensor_tensor_scan(cnt[:, 1, :], ones[:, 0:E], cnt[:, 0, :], 0.0, ALU.mult, ALU.add))
                link(nc.vector.tensor_tensor(cnt[:, 2, :], cnt[:, 1, :], cnt[:, 0, :], ALU.subtract))
                link(nc.vector.tensor_tensor(slotv, slotv,
                                             cnt[:, 2, :].unsqueeze(2).broadcast_to([P, E, J]), ALU.add))
                link(nc.vector.tensor_tensor(slotv, slotv,
                                             ps[:, HALF:HALF + E * J].rearrange("p (e j) -> p e j", e=E), ALU.add))
                for w in range(2):
                    link(nc.vector.tensor_tensor(hot[:, w, :, :], hot[:, w, :, :], slotv, ALU.mult))
                    link(nc.vector.tensor_reduce(slotf[:, w, :], hot[:, w, :, :].rearrange("p e j -> p j e"), AX, ALU.add))
                nc.vector.tensor_copy(slots[:, b, :, :], slotf[:, :, :]).then_inc(slots_ready, 1)
                link(nc.vector.tensor_tensor(cmp, t_iota[:, :, :],
                                             cnt[0:1, 1, :].unsqueeze(1).broadcast_to([1, TILES, E]), ALU.is_ge))
                link(nc.vector.tensor_reduce(tabf[:, :], cmp, AX, ALU.add))
                nc.vector.tensor_scalar_min(tab[0:1, b, :], tabf[:, :], float(E - 1)).then_inc(tab_ready, 1)

            layer1 = {"project": [v_project], "tokens": [v_tokens], "keys": [v_key_max], "query_value": [v_query_value],
                      "keyT": [v_query_max], "queries": [v_queries], "context": [v_context], "attend": [v_attend],
                      "norm": [v_norm], "norm2": [v_norm2], "logits": [v_gates], "route": [v_route],
                      "counts": [v_slots]}

            def expert_bias(e):
                if e == 0:
                    dve.wait_ge(ld_b1, 16)
                dve.wait_ge(bias_done, e + 1)
                nc.vector.tensor_tensor(bias1[:, e, :], bias1[:, e, :], bank(e % 2), ALU.add).then_inc(bias_added, 1)

            group_norm(0)
            group_norm(1)
            split(0)
            split(1)
            dve.wait_ge(vcol_sb, 2)
            for g in range(slots_by(0)):
                max_slot(g)
            for s in range(UNITS * STEPS):
                for g in range(slots_by(s), slots_by(s + 1)):
                    max_slot(g)
                if s % KT == 1 and s > KT:
                    normalise((s // KT - 1) // 2, (s // KT - 1) % 2)
                for e in BIAS_AT.get(s, ()):
                    expert_bias(e)
                if s == BEGIN_LAYER1:
                    dve.wait_ge(ld_rows, 16 * 4)
                    dve.wait_ge(consts_ready, 2)
                run_parts(layer1, LAYER1_AT, s, 0)
            normalise(UNITS - 1, 1)
            run_parts(layer1, LAYER1_AT_TILE, "before", 1)

            def experts(b):
                def x_copy(s, turn):
                    p = parity(b, s)
                    n = TILES * b + s + STRIDE * turn
                    dve.wait_ge(xT_ready, n + 1)
                    if TILES * b + s >= 2:
                        dve.wait_ge(h_ready, n - 1)
                    nc.vector.tensor_copy(XTT[:, p, :], bank(6 + p)[:, P:2 * P]).then_inc(xT_sb, 1)

                expert_of = {}

                def load_expert(s, turn):
                    key = (s, isinstance(turn, int))
                    if key not in expert_of:
                        expert_of[key] = dve.value_load(tab[0:1, b, bass.ds(s + STRIDE * turn, 1)], min_val=0,
                                                        max_val=E - 1)
                    return expert_of[key]

                def step(s, turn):
                    n = TILES * b + s + STRIDE * turn
                    if s == 0:
                        x_copy(0, 0)
                    if is_tile(s):
                        p = parity(b, s)
                        e = load_expert(s, turn)
                        dve.wait_ge(h_ready, n + 1)
                        if TILES * b + s >= 2:
                            dve.wait_ge(g_ready, n - 1)
                        nc.vector.tensor_tensor(H1[:, p, :], bank(2 + p), bias1[:, e, :], ALU.add).then_inc(h_sb, 1)
                    if is_tile(s + 1):
                        x_copy(s + 1, turn)
                    if is_tile(s - 2):
                        p = parity(b, s - 2)
                        e = load_expert(s - 2, turn)
                        dve.wait_ge(y_ready, n - 1)
                        before = earlier(b, s - 2, p)
                        if before:
                            dve.wait_ge(y_out[p], 16 * (before + STRIDE // 2 * turn))
                        nc.vector.tensor_tensor(Y[:, p, :], bank(6 + p)[:, 0:D], bias2[:, e, :],
                                                ALU.add).then_inc(y_sb, 1)

                dve.wait_ge(tab_ready, b + 1)
                expert_steps(dve, b, step, layer1)

            dve.wait_ge(ld_b2, 16)
            for b in range(B):
                experts(b)
            for b in range(B):
                for g in range(GROUPS):
                    dve.wait_ge(gathered[b][g], 16 * 4)
                    for w in range(2):
                        for j in (2 * g, 2 * g + 1):
                            t = t2[:, b, j, :]
                            last = nc.vector.scalar_tensor_tensor(t, YG[:, b, 2 * j + w, :], wts[:, b, j, w:w + 1], t,
                                                                  ALU.mult, ALU.add)
                        if w == 0:
                            link(last)
                    last.then_inc(mix_ready, 1)


_INS = ['x', 'L0_conv_gn_weight', 'L0_conv_gn_bias', 'L0_conv_qkv_weight', 'L0_conv_out_weight', 'L0_conv_out_bias',
        'L1_attn_Wk', 'L1_attn_bk', 'L1_attn_Wq', 'L1_attn_bq', 'L1_attn_Wv', 'L1_attn_bv', 'L1_attn_Wr', 'L1_attn_br',
        'L1_ffn_Wr', 'L1_ffn_br', 'L1_ffn_ln_g', 'L1_ffn_ln_b', 'L1_ffn_W1', 'L1_ffn_b1', 'L1_ffn_W2', 'L1_ffn_b2']
_OUT = ((2, 128, 32, 32), 'float32')


def kernel(**inputs):
    import numpy as _np
    import concourse.bacc as _bacc
    from concourse import mybir as _mybir
    from concourse.bass_utils import run_bass_kernel_spmd as _run

    nc = _bacc.Bacc("TRN2", target_bir_lowering=False, num_devices=1)
    arrays, args = {}, []
    for name in _INS:
        a = _np.ascontiguousarray(inputs[name])
        arrays[f"in_{name}"] = a
        args.append(nc.dram_tensor(f"in_{name}", a.shape, _mybir.dt.from_np(a.dtype), kind="ExternalInput").ap())
    shape, dtype = _OUT
    args.append(nc.dram_tensor("out_0", shape, _mybir.dt.from_np(_np.dtype(dtype)), kind="ExternalOutput").ap())
    build_program(nc, *args)
    r = _run(nc, [arrays], core_ids=[0])
    return r.results[0]["out_0"]
```

```python
import concourse.bass as bass
from concourse import mybir
from contextlib import ExitStack
from math import sqrt


def build_program(nc, x, gn_weight, gn_bias, qkv_weight, out_weight, out_bias, Wk, bk, Wq, bq, Wv, bv, Wr, br,
                  router_w, router_b, ln_g, ln_b, W1, b1, W2, b2, out):
    f32, f32r = mybir.dt.float32, mybir.dt.float32r
    i32, u32 = mybir.dt.int32, mybir.dt.uint32
    ALU, ACT, AX = mybir.AluOpType, mybir.ActivationFunctionType, mybir.AxisListType.X

    B, C, H_, W_ = x.shape
    L = H_ * W_
    P = 128
    J = L // P
    HALF = 512
    HEADS0, HD = 4, 32
    PAIRS = HEADS0 // 2
    UNITS = B * PAIRS
    QT, KT = L // P, L // P
    STEPS = 2 * KT
    SCORE_SCALE = 1.0 / sqrt(C)
    HEADS1, HK = 8, 16
    E, D, HID = W1.shape
    HC = HID // P
    TILES = (2 * L + E * (P - 1)) // P
    NT = B * TILES
    NB = 3
    EPS = 1e-5
    STORE_LAG = 9
    GROUPS = J // 2
    SPLIT = 3 * HD
    STACK = SPLIT + 2
    QH = QT // 2
    RING = 2 * 2 * QH + 1
    SLOTS = 2 * UNITS * RING

    xs = nc.dram_tensor("expert_in", (NT * P, D), f32).ap()
    ys = nc.dram_tensor("expert_out", (NT * P, D), f32).ap()

    ctx = ExitStack()
    with ctx:
        base = nc.sbuf_base
        room = [0]
        ctx.enter_context(nc.sbuf_tensor("slab", [P, 208 * 1024 - 512], mybir.dt.uint8))
        start = (base + 31) // 32 * 32

        def at(name, shape, dt, offset):
            size = 4
            for n in shape[1:]:
                size *= n
            return nc.alloc_sbuf_tensor_at(name, list(shape), dt, offset=start + offset), offset + size

        def sb(name, shape, dt=f32):
            t, end = at(name, shape, dt, room[0])
            room[0] = (end + 31) // 32 * 32
            return t

        def sem(name):
            return ctx.enter_context(nc.semaphore(name))

        w1 = sb("w1", [P, E, HID])
        bias1 = sb("bias1", [P, E, HID])
        w2 = sb("w2", [P, E, HC, D])
        bias2 = sb("bias2", [P, E, D])
        wT = sb("wT", [P, 8, P])
        vcol = sb("vcol", [P, 5 + 2 * E])
        bqv = sb("bqv", [P, 2, P])
        rw = sb("rw", [P, E])
        rb = sb("rb", [P, E])
        ident = sb("ident", [P, P])
        ones = sb("ones", [P, P])
        upper = sb("upper", [P, P])
        gmat = sb("gmat", [P, P])
        bmask = sb("bmask", [P, P])
        iota_e = sb("iota_e", [P, E])
        seg = sb("seg", [P, E, J])
        t_iota = sb("t_iota", [1, TILES, E])
        minus_half = sb("minus_half", [P, J])
        X = sb("X", [P, B, L])
        xn = sb("xn", [P, B, L])
        t2 = sb("t2", [P, B, J, P])
        X2 = sb("X2", [P, B, J, P])
        probs = sb("probs", [P, 3, 2 * HALF])
        vT = sb("vT", [P, B, KT, C])
        attn = sb("attn", [P, B, L])
        wrow = attn[:, 0, :].rearrange("p (j c) -> p j c", j=8)
        gn_row, vrow = attn[0:2, 1, 0:P], attn[0:3 + 2 * E, 1, P:2 * P]
        hl_at = room[0]
        q_hi, q_lo, k_hi, k_lo = ([sb(name, [P, L], f32r), at(name + "1", [P, L], f32r, 4 * L * i)[0]]
                                  for i, name in enumerate(("q_hi", "q_lo", "k_hi", "k_lo")))
        stack_at = room[0]
        Qs = sb("Qs", [P, B, HEADS0, L], f32r)
        Ks = sb("Ks", [P, B, HEADS0, L], f32r)
        QV, o = at("QV", [P, J, 2, P], f32, hl_at)
        QT_sb, o = at("QT_sb", [P, L], f32, o)
        F, o = at("F", [P, J, P], f32, o)
        assert o <= stack_at
        EK, EKT = xn[:, 0, :], xn[:, 1, :].rearrange("p (j k) -> p j k", j=J)
        CT, M1 = xn[:, 0, 0:P], xn[:, 0, P:2 * P]
        tot, incl, slotv = (xn[:, 0, 2 * P + i * E * J:2 * P + (i + 1) * E * J].rearrange("p (e j) -> p e j", e=E)
                            for i in range(3))
        hot = xn[:, 0, 4 * P:4 * P + 2 * E * J].rearrange("p (w e j) -> p w e j", w=2, e=E)
        cmp = xn[0:1, 0, 5 * P:5 * P + TILES * E].rearrange("p (t e) -> p t e", e=E)
        XR, o = at("XR", [P, NB, P], f32, stack_at)
        XTT, o = at("XTT", [P, NB, P], f32, o)
        H1, o = at("H1", [P, NB, HID], f32, o)
        G, o = at("G", [P, NB, HID], f32, o)
        GT, o = at("GT", [P, 2, HC, P], f32, o)
        Y, o = at("Y", [P, NB, D], f32, o)
        YG, o = at("YG", [P, B, 2 * J, D], f32, o)
        OUT, o = at("OUT", [P, B, L], f32, o)
        assert o <= stack_at + 2 * B * HEADS0 * L * 4
        gst = sb("gst", [P, B, 2, 6])
        gmv = sb("gmv", [P, B, 2])
        gtmp = sb("gtmp", [P, B, 4])
        ve = sb("ve", [P, 2 + 3 * B, J])
        rstd = sb("rstd", [P, 2 + 3 * B, J])
        lst = sb("lst", [P, J, 6])
        lmv = sb("lmv", [P, J, 2])
        pm = sb("pm", [P, 2, QH, 2])
        negm = sb("negm", [P, 2, QH])
        mhl = sb("mhl", [P, 2, 2, QH], f32r)
        mrow = sb("mrow", [4 * QH, P], f32r)
        rec = sb("rec", [64, HALF])
        sums = X2[0:64, 1, J // 2:, :].rearrange("p j c -> p (j c)")
        assert TILES * D // 2 <= (J + J // 2) * P
        rec16 = sb("rec16", [64, HALF // 32])
        kneg = sb("kneg", [P, 2])
        ksum = sb("ksum", [P, 2])
        qst = sb("qst", [P, J, HEADS1, 3])
        lg = sb("lg", [P, J, E])
        lst2 = sb("lst2", [P, J, 4])
        top = sb("top", [P, J, 8])
        topi = sb("topi", [P, J, 8], u32)
        topf = sb("topf", [P, J, 2])
        wts = sb("wts", [P, B, J, 2])
        mask = sb("mask", [P, E, J])
        cnt_i = sb("cnt_i", [P, E], i32)
        cnt = sb("cnt", [P, 3, E])
        slotf = sb("slotf", [P, 2, J])
        slots = sb("slots", [P, B, 2, J], u32)
        tabf = sb("tabf", [1, TILES])
        tab = sb("tab", [1, NT], i32)
        assert start + room[0] <= nc.sbuf_usable_end

        ps = ctx.enter_context(nc.psum_tensor("ps", [P, 8 * HALF], f32))

        def bank(i, n=1):
            return ps[:, i * HALF:(i + n) * HALF]

        ld_x = [sem(f"ld_x{b}") for b in range(B)]
        ld_wqkv, ld_w, ld_gn, ld_vec, ld_rows = sem("ld_wqkv"), sem("ld_w"), sem("ld_gn"), sem("ld_vec"), sem("ld_rows")
        ld_w1, ld_b1, ld_w2, ld_b2 = sem("ld_w1"), sem("ld_b1"), sem("ld_w2"), sem("ld_b2")
        stack_in = [sem(f"stack_in{u}") for u in range(UNITS)]
        stack_in_pool = sem("stack_in_pool")
        mrow_in = [sem(f"mrow_in{u}_{h}") for u in range(UNITS) for h in range(2)]
        ones_in, xs_zeroed = sem("ones_in"), sem("xs_zeroed")
        scattered = [sem(f"scattered{b}") for b in range(B)]
        gathered = [[sem(f"gathered{b}_{g}") for g in range(J // 2)] for b in range(B)]
        x_in = [sem(f"x_in{i}") for i in range(NB)]
        y_out = [sem(f"y_out{i}") for i in range(NB)]
        stored = sem("stored")
        dve_chain, pool_chain = sem("dve_chain"), sem("pool_chain")
        ident_ready, consts_ready = sem("ident_ready"), sem("consts_ready")
        wT_ready, wT_sb = sem("wT_ready"), sem("wT_sb")
        vcol_ready, vcol_sb = sem("vcol_ready"), sem("vcol_sb")
        gn_in, gn_out = sem("gn_in"), sem("gn_out")
        var_ready, rstd_ready = sem("var_ready"), sem("rstd_ready")
        xn_ready, resid_ready = sem("xn_ready"), sem("resid_ready")
        qkv_ready, hi_ready, qk_split, v_sb = sem("qkv_ready"), sem("hi_ready"), sem("qk_split"), sem("v_sb")
        slot_ready, slot_used = sem("slot_ready"), sem("slot_used")
        mhl_ready, mrow_ready = sem("mhl_ready"), sem("mrow_ready")
        st_ready, exp_done, pv_done, o_used = sem("st_ready"), sem("exp_done"), sem("pv_done"), sem("o_used")
        proj_ready, t_sb, F_ready = sem("proj_ready"), sem("t_sb"), sem("F_ready")
        keys_ready, kneg_ready, ek_ready = sem("keys_ready"), sem("kneg_ready"), sem("ek_ready")
        qv_ready, qv_sb = sem("qv_ready"), sem("qv_sb")
        ekT_ready, ekT_sb = sem("ekT_ready"), sem("ekT_sb")
        qsub_ready, qexp_ready, qn_ready = sem("qsub_ready"), sem("qexp_ready"), sem("qn_ready")
        ctx_ready, ct_sb, m1_ready, m1_sb = sem("ctx_ready"), sem("ct_sb"), sem("m1_ready"), sem("m1_sb")
        qT_ready, qT_sb, att_ready, n2_ready = sem("qT_ready"), sem("qT_sb"), sem("att_ready"), sem("n2_ready")
        n2T_ready, n2T_sb, lg_ready = sem("n2T_ready"), sem("n2T_sb"), sem("lg_ready")
        lsub_ready, lexp_ready = sem("lsub_ready"), sem("lexp_ready")
        mask_ready, cum_ready, slots_ready, tab_ready = sem("mask_ready"), sem("cum_ready"), sem("slots_ready"), sem("tab_ready")
        x2_ready = sem("x2_ready")
        xT_ready, xT_sb, h_ready, h_sb = sem("xT_ready"), sem("xT_sb"), sem("h_ready"), sem("h_sb")
        g_ready, gT_ready, gT_sb = sem("g_ready"), sem("gT_ready"), sem("gT_sb")
        y_ready, y_sb = sem("y_ready"), sem("y_sb")
        mix_ready, outT_ready, out_sb = sem("mix_ready"), sem("outT_ready"), sem("out_sb")

        def head(u, hd):
            return 2 * (u % PAIRS) + hd

        SP_LOADS = 2
        GN_BANK = (3, 1)
        QV_BANK = ((0, 0), (2, 4))

        STRIDE = 2 * NB
        TURNS = (TILES - 5) // STRIDE
        LOOP_FROM = NT - 2 - STRIDE * TURNS
        LOOP_TO = LOOP_FROM + STRIDE * TURNS
        LAST = NT + 3
        assert LOOP_FROM - 3 >= TILES

        order = [(k, i) for k in range(2 * UNITS) for i in range(RING - 1)]
        for k in range(2 * UNITS):
            order.insert(min(RING * (k + 1) + 1, len(order)), (k, "rows"))
        assert len(order) == SLOTS
        place = {slot: g for g, slot in enumerate(order)}

        AHEAD = RING + 12

        def slots_by(s):
            return min(SLOTS, AHEAD + -(-(SLOTS - AHEAD) * s // (2 * STEPS)))

        BEGIN_LAYER1 = 2 * STEPS + 1
        LAYER1_AT = {BEGIN_LAYER1: "residual", 34: "project", 35: "tokens_stats", 37: "tokens", 40: "keys",
                     41: "keys_exp", 42: "query_value0", 43: "query_value1", 45: "keyT", 46: "queries_exp",
                     47: "queries queries_scaled context", 48: "fold", 49: "queryT", 50: "queryT_sb",
                     51: "attend stats", 53: "norm stats2", 55: "tokenT", 56: "tokenT_sb", 57: "logits",
                     58: "gates_exp norm2", 59: "route choose", 60: "counts"}
        LAYER1_AT_TILE = {"before": "residual project tokens_stats tokens keys keys_exp query_value0 query_value1",
                          0: "keyT queries_exp", 2: "queries queries_scaled context", 3: "fold",
                          4: "queryT queryT_sb", 5: "attend stats", 6: "norm", 7: "stats2 tokenT",
                          8: "tokenT_sb norm2", 9: "logits", 10: "gates_exp", 11: "route choose", 12: "counts"}

        def run_parts(parts, where, step, b):
            for name in where.get(step, "").split():
                for part in parts.get(name, []):
                    part(b)

        def expert_steps(engine, step, layer1):
            for s in range(LOOP_FROM):
                step(s, 0)
                run_parts(layer1, LAYER1_AT_TILE, s, 1)
            with engine.Fori(0, TURNS) as turn:
                for s in range(LOOP_FROM, LOOP_FROM + STRIDE):
                    step(s, turn)
            for s in range(LOOP_TO, LAST):
                step(s, 0)

        def is_tile(t):
            return 0 <= t < NT

        def stack_loads(u, hd):
            b, n = u // PAIRS, head(u, hd)
            return [(st[r * HD:(r + 1) * HD, b, n, :].bitcast(f32), part[n * HD:(n + 1) * HD, :].bitcast(f32))
                    for st, parts in ((Qs, (q_hi[b], q_hi[b], q_lo[b])), (Ks, (k_hi[b], k_lo[b], k_hi[b])))
                    for r, part in enumerate(parts)]

        block = ctx.enter_context(nc.Block())

        @block.sync
        def _(sp):
            sp.dma_start(X[:, 0, :], x[0].rearrange("c h w -> c (h w)")).then_inc(ld_x[0], 16)
            for i, v in enumerate((gn_weight, gn_bias)):
                sp.dma_start(gn_row[i:i + 1, :], v.rearrange("(a c) -> a c", a=1)).then_inc(ld_gn, 16)
            sp.dma_start(X[:, 1, :], x[1].rearrange("c h w -> c (h w)")).then_inc(ld_x[1], 16)
            for i, v in enumerate((out_bias, bk, br)):
                sp.dma_start(vrow[i:i + 1, :], v.rearrange("(a c) -> a c", a=1)).then_inc(ld_vec, 16)
            for i, v in enumerate((ln_g, ln_b)):
                sp.dma_start(vrow[3 + i * E:3 + (i + 1) * E, :], v).then_inc(ld_vec, 16)
            sp.dma_start(bqv[:, 0, :], bq.rearrange("(a c) -> a c", a=1).broadcast_to([P, P])).then_inc(ld_rows, 16)
            sp.dma_start(bqv[:, 1, :], bv.rearrange("(a c) -> a c", a=1).broadcast_to([P, P])).then_inc(ld_rows, 16)
            sp.dma_start(rb[:, :], router_b.rearrange("(a c) -> a c", a=1).broadcast_to([P, E])).then_inc(ld_rows, 16)
            sp.dma_start(rw[:, :], router_w).then_inc(ld_rows, 16)
            sp.wait_ge(consts_ready, 1)
            sp.dma_start(Ks[SPLIT:STACK, :, :, :].bitcast(f32).rearrange("s b n (t q) -> s (b n t) q", q=P),
                         ones[:, :]).then_inc(ones_in, 16)

            def stacks(u):
                b = u // PAIRS
                sp.wait_ge(hi_ready, 2 * b + 2)
                sp.wait_ge(qk_split, 2 * b + 2)
                for hd in range(2):
                    for dst, src in stack_loads(u, hd)[0:SP_LOADS if u == 0 and hd else None]:
                        sp.dma_start(dst, src).then_inc(stack_in[u], 16)

            def max_rows(u, qh):
                b, k = u // PAIRS, 2 * u + qh
                sp.wait_ge(mrow_ready, k + 1)
                for hd in range(2):
                    dst = Qs[SPLIT:STACK, b, head(u, hd), qh * HALF:(qh + 1) * HALF]
                    sp.dma_start(dst.bitcast(f32).rearrange("s (t q) -> s t q", t=QH),
                                 mrow[hd * 2 * QH:(hd + 1) * 2 * QH, :].bitcast(f32)).then_inc(mrow_in[k], 16)

            stacks(0)
            stacks(1)
            max_rows(0, 0)
            stacks(2)
            stacks(3)
            for u in range(PAIRS, UNITS):
                sp.wait_ge(stack_in[u], 16 * 12)
            sp.dma_start(w1[:, :, :], W1.rearrange("e d h -> d e h")).then_inc(ld_w1, 16)
            max_rows(0, 1)
            sp.dma_start(bias1[:, :, :].rearrange("p e h -> p (e h)"),
                         b1.rearrange("(a e) h -> a (e h)", a=1).broadcast_to([P, E * HID])).then_inc(ld_b1, 16)
            max_rows(1, 0)
            for e in range(E):
                sp.dma_start(w2[:, e, :, :], W2[e].rearrange("(c p) d -> p c d", p=P)).then_inc(ld_w2, 16)
            sp.dma_start(bias2[:, :, :].rearrange("p e h -> p (e h)"),
                         b2.rearrange("(a e) h -> a (e h)", a=1).broadcast_to([P, E * D])).then_inc(ld_b2, 16)
            for k in range(3, 2 * UNITS):
                max_rows(k // 2, k % 2)

            def move_tiles(s, turn):
                t = s + NB * turn
                if is_tile(s):
                    p = s % NB
                    if s >= NB:
                        sp.wait_ge(xT_ready, t - NB + 1)
                    sp.dma_start(XR[:, p, :], xs[bass.ts(t, P), :]).then_inc(x_in[p], 16)
                if is_tile(s - STORE_LAG):
                    p = (s - STORE_LAG) % NB
                    sp.wait_ge(y_sb, t - STORE_LAG + 1)
                    sp.dma_start(ys[bass.ts(t - STORE_LAG, P), :], Y[:, p, :]).then_inc(y_out[p], 16)

            for b in range(B):
                sp.wait_ge(scattered[b], 16 * 2 * J)
                first, end = (STORE_LAG, TILES) if b == 0 else (TILES, NT)
                turns = (end - first) // NB
                if b == 0:
                    for s in range(first):
                        move_tiles(s, 0)
                with sp.Fori(0, turns) as turn:
                    for s in range(first, first + NB):
                        move_tiles(s, turn)
                for s in range(first + NB * turns, end):
                    move_tiles(s, 0)
            for s in range(NT, NT + STORE_LAG):
                move_tiles(s, 0)
            for b in range(B):
                sp.wait_ge(out_sb, GROUPS * (b + 1))
                sp.dma_start(out[b].rearrange("c h w -> c (h w)"), OUT[:, b, :]).then_inc(stored, 16)
            sp.wait_ge(stored, 16 * B)

        @block.gpsimd
        def _(pool):
            chain = [0]

            def link(ins):
                chain[0] += 1
                ins.then_inc(pool_chain, 1)
                pool.wait_ge(pool_chain, chain[0])

            def select(t, pattern, base_, mult, op, fill):
                link(nc.gpsimd.affine_select(out=t, in_=t, compare_op=op, fill=fill, base=base_, pattern=pattern,
                                             channel_multiplier=mult))

            link(nc.gpsimd.memset(ident[:, :], 0.0))
            select(ident[:, :], [[-1, P]], 0, 1, ALU.not_equal, 1.0)
            nc.gpsimd.memset(minus_half[:, :], -0.5).then_inc(ident_ready, 1)

            def blocks(t, value, size):
                link(nc.gpsimd.memset(t[:, :], value))
                v = t[:, :].rearrange("p (g i) -> p g i", i=size)
                select(v, [[-size, P // size], [0, size]], 0, 1, ALU.is_ge, 0.0)
                select(v, [[size, P // size], [0, size]], size - 1, -1, ALU.is_ge, 0.0)

            blocks(gmat, 1.0 / 8, 8)
            nc.gpsimd.memset(ones[:, :], 1.0).then_inc(consts_ready, 1)

            def rsqrt(i):
                n = 1 if i < B else J
                pool.wait_ge(var_ready, i + 1)
                nc.gpsimd.tensor_tensor(rstd[:, i, 0:n], ve[:, i, 0:n], minus_half[:, 0:n], ALU.pow).then_inc(rstd_ready, 1)

            rsqrt(0)
            rsqrt(1)
            pool.wait_ge(hi_ready, 2)
            pool.wait_ge(qk_split, 2)
            for dst, src in stack_loads(0, 1)[SP_LOADS:]:
                pool.dma_start(dst, src).then_inc(stack_in_pool, 16)
            pool.wait_ge(vcol_sb, 2)
            for b in range(B):
                pool.wait_ge(xn_ready, b + 1)
                nc.gpsimd.tensor_scalar(X[:, b, :], X[:, b, :], vcol[:, 2:3], None, ALU.add).then_inc(resid_ready, 1)
            blocks(bmask, 1.0, HK)
            link(nc.gpsimd.memset(upper[:, :], 1.0))
            select(upper[:, :], [[1, P]], 0, -1, ALU.is_gt, 0.0)
            nc.gpsimd.iota(iota_e[:, :], [[1, E]], base=0, channel_multiplier=0,
                           allow_small_or_imprecise_dtypes=True)
            nc.gpsimd.iota(t_iota[:, :, :], [[P, TILES], [0, E]], base=0, channel_multiplier=0,
                           allow_small_or_imprecise_dtypes=True)
            link(nc.gpsimd.memset(seg[:, :, :], 1.0))
            nc.gpsimd.memset(seg[:, :, 0:1], 0.0).then_inc(consts_ready, 1)
            per = TILES * D // 2
            zeros = X2[:, :, :, :].rearrange("p b j d -> p (b j d)")[:, 0:per]
            link(nc.gpsimd.memset(zeros, 0.0))
            pool.wait_ge(mhl_ready, 1)
            for b in range(B):
                v = xs[b * TILES * P:(b + 1) * TILES * P, :].rearrange("(p r) d -> p (r d)", p=P)
                for i in range(2):
                    pool.dma_start(v[:, i * per:(i + 1) * per], zeros).then_inc(xs_zeroed, 16)
            pool.wait_ge(xs_zeroed, 16 * 2 * B)

            def scatter(b, between):
                pool.wait_ge(slots_ready, b + 1)
                pool.wait_ge(x2_ready, b + 1)
                for j in range(J):
                    between(j)
                    for w in range(2):
                        pool.indirect_dma_start(xs[:, :], bass.IndirectOffsetOnAxis(ap=slots[:, b, w, j:j + 1], axis=0),
                                                X2[:, b, j, :], None).then_inc(scattered[b], 16)

            def gather(b):
                for p in range(NB):
                    pool.wait_ge(y_out[p], 16 * len(range(p, TILES * (b + 1), NB)))
                for j in range(J):
                    for w in range(2):
                        pool.indirect_dma_start(YG[:, b, 2 * j + w, :], None, ys[0:(b + 1) * TILES * P, :],
                                                bass.IndirectOffsetOnAxis(ap=slots[:, b, w, j:j + 1], axis=0)
                                                ).then_inc(gathered[b][j // 2], 16)

            rsqrt(B)
            rsqrt(B + 1)
            rsqrt(B + 2)
            scatter(0, lambda j: rsqrt(B + 3) if j == J - 2 else None)
            rsqrt(B + 4)
            rsqrt(B + 5)
            scatter(1, lambda j: None)
            for b in range(B):
                gather(b)

        @block.scalar
        def _(act):
            for n in range(HEADS0):
                src = qkv_weight[n * SPLIT:(n + 1) * SPLIT, :].rearrange("(s i) c -> i s c", s=3)
                act.dma_start(wrow[n * HD:(n + 1) * HD, 0:3, :], src).then_inc(ld_wqkv, 16)
            for n, w in enumerate((out_weight, Wq, Wv, Wk, Wr)):
                act.dma_start(wrow[:, 3 + n, :], w).then_inc(ld_w, 16)
            act.wait_ge(wT_ready, 1)
            nc.scalar.activation(wT[:, 0:3, :], ps[:, 0:3 * P].rearrange("p (j c) -> p j c", j=3),
                                 ACT.Copy).then_inc(wT_sb, 1)

            def split(b):
                act.wait_ge(qkv_ready, 3 * b + 1)
                nc.scalar.activation(q_hi[b][:, :], bank(4, 2), ACT.Copy, scale=SCORE_SCALE).then_inc(hi_ready, 1)
                act.wait_ge(qkv_ready, 3 * b + 2)
                nc.scalar.activation(k_hi[b][:, :], bank(6, 2), ACT.Copy).then_inc(hi_ready, 1)
                act.wait_ge(qkv_ready, 3 * b + 3)
                nc.scalar.activation(vT[:, b, :, :].rearrange("p t c -> p (t c)"), bank(2, 2), ACT.Copy).then_inc(v_sb, 1)

            def exps(u, step):
                s = u * STEPS + step
                act.wait_ge(st_ready, s + 1)
                if s >= 3:
                    act.wait_ge(pv_done, s - 2)
                nc.scalar.activation(probs[:, s % 3, :], bank(2 + 2 * (s % 2), 2), ACT.Exp).then_inc(exp_done, 1)

            def a_tokens(b):
                act.wait_ge(proj_ready, b + 1)
                nc.scalar.activation(t2[:, b, :, :].rearrange("p j c -> p (j c)"), bank(2 * b, 2),
                                     ACT.Copy).then_inc(t_sb, 1)

            def a_key_exp(b):
                act.wait_ge(kneg_ready, b + 1)
                nc.scalar.activation(EK, bank(0, 2), ACT.Exp, bias=kneg[:, 1:2],
                                     accum_out=ksum[:, 0:1]).then_inc(ek_ready, 1)

            def a_keyT(b):
                act.wait_ge(ekT_ready, b + 1)
                nc.scalar.activation(xn[:, 1, :], bank(0, 2), ACT.Copy).then_inc(ekT_sb, 1)

            def a_query_exp(b):
                act.wait_ge(qsub_ready, b + 1)
                q = QV[:, :, 0, :]
                nc.scalar.activation(q, q, ACT.Exp).then_inc(qexp_ready, 1)

            def a_queryT(b):
                act.wait_ge(qT_ready, b + 1)
                nc.scalar.activation(QT_sb[:, :], bank(0, 2), ACT.Copy).then_inc(qT_sb, 1)

            def a_tokenT(b):
                act.wait_ge(n2T_ready, b + 1)
                nc.scalar.activation(QT_sb[:, :], bank(0, 2), ACT.Copy).then_inc(n2T_sb, 1)

            def a_route(b):
                act.wait_ge(lsub_ready, b + 1)
                nc.scalar.activation(lg[:, :, :], lg[:, :, :], ACT.Exp).then_inc(lexp_ready, 1)

            layer1 = {"tokens_stats": [a_tokens], "keys_exp": [a_key_exp], "queries_exp": [a_keyT, a_query_exp],
                      "queryT_sb": [a_queryT], "tokenT_sb": [a_tokenT], "gates_exp": [a_route]}

            split(0)
            act.wait_ge(wT_ready, 2)
            nc.scalar.activation(wT[:, 3:8, :], ps[:, 0:5 * P].rearrange("p (j c) -> p j c", j=5),
                                 ACT.Copy).then_inc(wT_sb, 1)
            nc.scalar.activation(vcol[:, 2:], ps[:, 5 * P:5 * P + 3 + 2 * E], ACT.Copy).then_inc(vcol_sb, 1)
            split(1)
            for s in range(UNITS * STEPS):
                exps(s // STEPS, s % STEPS)
                run_parts(layer1, LAYER1_AT, s, 0)
            run_parts(layer1, LAYER1_AT_TILE, "before", 1)

            def expert_step(s, turn):
                n = s + STRIDE * turn
                if is_tile(s):
                    p = s % NB
                    act.wait_ge(h_sb, n + 1)
                    if s >= NB:
                        act.wait_ge(gT_ready, n - 2)
                    nc.scalar.activation(G[:, p, :], H1[:, p, :], ACT.Gelu).then_inc(g_ready, 1)
                if is_tile(s - 2):
                    p = s % 2
                    act.wait_ge(gT_ready, n - 1)
                    if s >= 4:
                        act.wait_ge(y_ready, n - 3)
                    nc.scalar.activation(GT[:, p, :, :].rearrange("p c t -> p (c t)"), bank(4 + p),
                                         ACT.Copy).then_inc(gT_sb, 1)

            expert_steps(act, expert_step, layer1)
            for b in range(B):
                v = OUT[:, b, :].rearrange("c (d j) -> c d j", j=J)
                for g in range(GROUPS):
                    k = GROUPS * b + g
                    act.wait_ge(outT_ready, k + 1)
                    nc.scalar.activation(v[:, :, 2 * g:2 * g + 2],
                                         bank(k % 2)[:, 0:2 * P].rearrange("c (j d) -> c d j", j=2),
                                         ACT.Copy).then_inc(out_sb, 1)

        @block.tensor
        def _(pe):
            pe.wait_ge(ident_ready, 1)
            pe.wait_ge(ld_gn, 16 * 2)
            nc.tensor.transpose(ps[:, 2 * HALF:2 * HALF + 2], gn_row, ident[0:2, 0:2]).then_inc(vcol_ready, 1)
            pe.wait_ge(ld_wqkv, 16 * HEADS0)
            for j in range(3):
                last = nc.tensor.transpose(ps[:, j * P:(j + 1) * P], wrow[:, j, :], ident[:, :])
            last.then_inc(wT_ready, 1)

            def weight_transposes():
                pe.wait_ge(ld_w, 16 * 5)
                pe.wait_ge(ld_vec, 16 * 5)
                pe.wait_ge(var_ready, B)
                for j in range(5):
                    nc.tensor.transpose(ps[:, j * P:(j + 1) * P], wrow[:, 3 + j, :], ident[:, :])
                n = 3 + 2 * E
                nc.tensor.transpose(ps[:, 5 * P:5 * P + n], vrow, ident[0:n, 0:n]).then_inc(wT_ready, 1)

            def group_stats(b, i):
                pe.wait_ge(gn_in, 2 * b + i + 1)
                if not (b or i):
                    pe.wait_ge(consts_ready, 1)
                src = gmv[:, b, 0:1] if i == 0 else gtmp[:, b, 1:2]
                nc.tensor.matmul(bank(GN_BANK[b])[:, i:i + 1], gmat[:, :], src,
                                 start=True, stop=True).then_inc(gn_out, 1)

            def queries_keys(b):
                pe.wait_ge(xn_ready, b + 1)
                if b == 0:
                    pe.wait_ge(wT_sb, 1)
                for i, at_ in ((0, 4), (1, 6)):
                    if b:
                        pe.wait_ge(qk_split, i + 1)
                    for h in range(2):
                        last = nc.tensor.matmul(bank(at_ + h), wT[:, i, :], xn[:, b, h * HALF:(h + 1) * HALF],
                                                start=True, stop=True)
                    last.then_inc(qkv_ready, 1)

            def values_of(b):
                if b == 0:
                    pe.wait_ge(vcol_sb, 1)
                else:
                    pe.wait_ge(v_sb, b)
                for t in range(KT):
                    last = nc.tensor.matmul(ps[:, 2 * HALF + t * P:2 * HALF + (t + 1) * P],
                                            xn[:, b, t * P:(t + 1) * P], wT[:, 2, :], start=True, stop=True)
                last.then_inc(qkv_ready, 1)

            def max_slot(g):
                k, i = order[g]
                u, qh = k // 2, k % 2
                b = u // PAIRS
                if i == 0 and qh == 0:
                    if u == 0:
                        pe.wait_ge(stack_in[u], 16 * (6 + SP_LOADS))
                        pe.wait_ge(stack_in_pool, 16 * (6 - SP_LOADS))
                    else:
                        pe.wait_ge(stack_in[u], 16 * 12)
                if g >= 2:
                    pe.wait_ge(slot_used, g - 1)
                elif g == 0:
                    pe.wait_ge(wT_sb, 2)
                    pe.wait_ge(vcol_sb, 2)
                if i != "rows":
                    hd, t, h = i // (2 * QH), QH * qh + (i // 2) % QH, i % 2
                    n = head(u, hd)
                    last = nc.tensor.matmul(bank(g % 2), Qs[0:SPLIT, b, n, t * P:(t + 1) * P],
                                            Ks[0:SPLIT, b, n, h * HALF:(h + 1) * HALF], start=True, stop=True)
                else:
                    pe.wait_ge(mhl_ready, k + 1)
                    last = nc.tensor.transpose(ps[0:4 * QH, (g % 2) * HALF:(g % 2) * HALF + P],
                                               mhl[:, :, :, :].bitcast(f32).rearrange("p h s t -> p (h s t)"), ident[:, :])
                last.then_inc(slot_ready, 1)

            def scores(u, step, hd):
                s = u * STEPS + step
                b, qh, kt = u // PAIRS, step // KT, step % KT
                if kt == 0 and hd == 0:
                    pe.wait_ge(mrow_in[2 * u + qh], 16 * 2)
                if s >= 2 and hd == 0:
                    pe.wait_ge(exp_done, s - 1)
                elif hd == 0:
                    pe.wait_ge(v_sb, B)
                    pe.wait_ge(qk_split, 2 * B)
                    pe.wait_ge(ones_in, 16)
                n = head(u, hd)
                last = nc.tensor.matmul(bank(2 + 2 * (s % 2) + hd), Ks[0:STACK, b, n, kt * P:(kt + 1) * P],
                                        Qs[0:STACK, b, n, qh * HALF:(qh + 1) * HALF], start=True, stop=True)
                if hd:
                    last.then_inc(st_ready, 1)

            def values(u, step, hd):
                s = u * STEPS + step
                b, qh, kt = u // PAIRS, step // KT, step % KT
                o = 2 * u + qh
                if hd == 0:
                    pe.wait_ge(exp_done, s + 1)
                    if kt == 0 and o >= 2:
                        pe.wait_ge(o_used, o - 1)
                n = head(u, hd)
                for i, w in ((hd, vT[:, b, kt, n * HD:(n + 1) * HD]), (2 + hd, ones[:, 0:HD])):
                    last = nc.tensor.matmul(bank(6 + o % 2)[i * HD:(i + 1) * HD, :], w,
                                            probs[:, s % 3, hd * HALF:(hd + 1) * HALF],
                                            start=kt == 0, stop=kt == KT - 1)
                if hd:
                    last.then_inc(pv_done, 1)

            def t_residual(b):
                pe.wait_ge(resid_ready, b + 1)
                if b == 0:
                    pe.wait_ge(slot_used, SLOTS)
                else:
                    pe.wait_ge(exp_done, UNITS * STEPS - 1)
                for j in range(J):
                    nc.tensor.matmul(bank(2 * b, 2)[:, j * P:(j + 1) * P], X[:, b, j::J], ident[:, :],
                                     start=j % 4 == 0, stop=False)

            def t_project(b):
                pe.wait_ge(o_used, 4 * b + 4)
                for j in range(J):
                    last = nc.tensor.matmul(bank(2 * b, 2)[:, j * P:(j + 1) * P], attn[:, b, j::J], wT[:, 3, :],
                                            start=False, stop=j % 4 == 3)
                last.then_inc(proj_ready, 1)

            def t_keys(b):
                pe.wait_ge(F_ready, b + 1)
                if b:
                    pe.wait_ge(slots_ready, b)
                for h in range(2):
                    last = nc.tensor.matmul(bank(h), wT[:, 6, :], F[:, 4 * h:4 * h + 4, :].rearrange("d j c -> d (j c)"),
                                            start=True, stop=True)
                last.then_inc(keys_ready, 1)

            def t_query_value(b, h):
                if b == 0:
                    if h == 0:
                        pe.wait_ge(ek_ready, b + 1)
                    else:
                        pe.wait_ge(qv_sb, 2 * b + h)
                for i in range(J // 2):
                    last = nc.tensor.matmul(bank(QV_BANK[b][h], 2)[:, i * 2 * P:(i + 1) * 2 * P], F[:, 4 * h + i, :],
                                            wT[:, 4:6, :].rearrange("d w k -> d (w k)"), start=True, stop=True)
                last.then_inc(qv_ready, 1)

            def t_keyT(b):
                pe.wait_ge(ek_ready, b + 1)
                pe.wait_ge(qv_sb, 2 * b + 2)
                for j in range(J):
                    last = nc.tensor.transpose(ps[:, j * P:(j + 1) * P], EK[:, j * P:(j + 1) * P], ident[:, :])
                last.then_inc(ekT_ready, 1)

            def t_context(b):
                pe.wait_ge(ekT_sb, b + 1)
                for j in range(J):
                    last = nc.tensor.matmul(ps[:, 0:P], QV[:, j, 1, :], EKT[:, j, :], start=j == 0, stop=j == J - 1)
                last.then_inc(ctx_ready, 1)

            def t_fold(b):
                pe.wait_ge(ct_sb, b + 1)
                nc.tensor.matmul(ps[:, HALF:HALF + P], CT, wT[:, 7, :], start=True, stop=True).then_inc(m1_ready, 1)

            def t_queryT(b):
                pe.wait_ge(qn_ready, b + 1)
                pe.wait_ge(m1_sb, b + 1)
                for j in range(J):
                    last = nc.tensor.transpose(ps[:, j * P:(j + 1) * P], QV[:, j, 0, :], ident[:, :])
                last.then_inc(qT_ready, 1)

            def t_attend(b):
                pe.wait_ge(qT_sb, b + 1)
                for h in range(2):
                    last = nc.tensor.matmul(bank(h), M1, QT_sb[:, h * HALF:(h + 1) * HALF], start=True, stop=True)
                last.then_inc(att_ready, 1)

            def t_tokenT(b):
                pe.wait_ge(n2_ready, b + 1)
                for j in range(J):
                    last = nc.tensor.transpose(ps[:, j * P:(j + 1) * P], F[:, j, :], ident[:, :])
                last.then_inc(n2T_ready, 1)

            def t_logits(b):
                pe.wait_ge(n2T_sb, b + 1)
                for j in range(J):
                    last = nc.tensor.matmul(ps[:, j * E:(j + 1) * E], QT_sb[:, j * P:(j + 1) * P], rw[:, :],
                                            start=True, stop=True)
                last.then_inc(lg_ready, 1)

            def t_counts(b):
                pe.wait_ge(mask_ready, b + 1)
                m = mask[:, :, :].rearrange("p e j -> p (e j)")
                nc.tensor.matmul(ps[:, HALF:HALF + E * J], upper[:, :], m, start=True, stop=True)
                nc.tensor.matmul(ps[:, HALF + E * J:HALF + 2 * E * J], ones[:, :], m, start=True,
                                 stop=True).then_inc(cum_ready, 1)

            layer1 = {"residual": [t_residual], "project": [t_project], "keys": [t_keys], "keyT": [t_keyT],
                      "query_value0": [lambda b: t_query_value(b, 0)], "query_value1": [lambda b: t_query_value(b, 1)],
                      "context": [t_context], "fold": [t_fold], "queryT": [t_queryT], "attend": [t_attend], "tokenT": [t_tokenT],
                      "logits": [t_logits], "counts": [t_counts]}

            group_stats(0, 0)
            group_stats(0, 1)
            queries_keys(0)
            group_stats(1, 0)
            values_of(0)
            group_stats(1, 1)
            weight_transposes()
            queries_keys(1)
            values_of(1)
            for g in range(slots_by(0)):
                max_slot(g)
            for hd in range(2):
                scores(0, 0, hd)
            for s in range(UNITS * STEPS):
                new = range(slots_by(s), slots_by(s + 1))

                def max_slots(quarter):
                    for g in new[len(new) * quarter // 4:len(new) * (quarter + 1) // 4]:
                        max_slot(g)

                for hd in range(2):
                    if s + 1 < UNITS * STEPS:
                        scores((s + 1) // STEPS, (s + 1) % STEPS, hd)
                    max_slots(hd)
                if s == BEGIN_LAYER1:
                    pe.wait_ge(consts_ready, 2)
                    pe.wait_ge(ld_rows, 16 * 4)
                run_parts(layer1, LAYER1_AT, s, 0)
                for hd in range(2):
                    values(s // STEPS, s % STEPS, hd)
                    max_slots(2 + hd)
            run_parts(layer1, LAYER1_AT_TILE, "before", 1)

            def x_transpose(s, turn):
                n = s + STRIDE * turn
                pe.wait_ge(x_in[s % NB], 16 * (s // NB + 1 + STRIDE // NB * turn))
                if s == 0:
                    pe.wait_ge(o_used, 2 * UNITS)
                if s >= 6:
                    pe.wait_ge(y_sb, n - 5)
                nc.tensor.transpose(bank(6 + s % 2)[:, P:2 * P], XR[:, s % NB, :], ident[:, :]).then_inc(xT_ready, 1)

            expert_of = {}

            def load_expert(s, turn):
                key = (s, isinstance(turn, int))
                if key not in expert_of:
                    if s in (0, TILES):
                        pe.wait_ge(tab_ready, s // TILES + 1)
                    expert_of[key] = pe.value_load(tab[0:1, bass.ds(s + STRIDE * turn, 1)], min_val=0, max_val=E - 1)
                return expert_of[key]

            def expert_step(s, turn):
                n = s + STRIDE * turn
                if s == 0:
                    x_transpose(0, 0)
                    x_transpose(1, 0)
                if is_tile(s):
                    e = load_expert(s, turn)
                    pe.wait_ge(xT_sb, n + 1)
                    nc.tensor.matmul(bank(2 + s % 2), XTT[:, s % NB, :], w1[:, e, :], start=True,
                                     stop=True).then_inc(h_ready, 1)
                if is_tile(s - 2):
                    pe.wait_ge(g_ready, n - 1)
                    for c in range(HC):
                        last = nc.tensor.transpose(bank(4 + s % 2)[:, c * P:(c + 1) * P],
                                                   G[:, (s - 2) % NB, c * P:(c + 1) * P], ident[:, :])
                    last.then_inc(gT_ready, 1)
                if is_tile(s + 1):
                    load_expert(s + 1, turn)
                if is_tile(s + 2):
                    x_transpose(s + 2, turn)
                if is_tile(s - 3):
                    p = (s - 3) % 2
                    e = load_expert(s - 3, turn)
                    pe.wait_ge(gT_sb, n - 2)
                    if is_tile(s + 1):
                        pe.wait_ge(xT_sb, n + 2)
                    else:
                        pe.wait_ge(y_sb, n - 4)
                    for c in range(HC):
                        last = nc.tensor.matmul(bank(6 + p)[:, 0:D], GT[:, p, c, :], w2[:, e, c, :], start=c == 0,
                                                stop=c == HC - 1)
                    last.then_inc(y_ready, 1)

            pe.wait_ge(ld_w1, 16)
            pe.wait_ge(ld_w2, 16 * E)
            expert_steps(pe, expert_step, layer1)
            pe.wait_ge(slots_ready, B)
            for b in range(B):
                for g in range(GROUPS):
                    k = GROUPS * b + g
                    pe.wait_ge(mix_ready, k + 1)
                    if k >= 2:
                        pe.wait_ge(out_sb, k - 1)
                    for j in range(2):
                        last = nc.tensor.transpose(bank(k % 2)[:, j * P:(j + 1) * P], t2[:, b, 2 * g + j, :], ident[:, :])
                    last.then_inc(outT_ready, 1)

        @block.vector
        def _(dve):
            chain = [0]

            def link(ins):
                chain[0] += 1
                ins.then_inc(dve_chain, 1)
                dve.wait_ge(dve_chain, chain[0])

            dve.wait_ge(vcol_ready, 1)
            nc.vector.tensor_copy(vcol[:, 0:2], ps[:, 2 * HALF:2 * HALF + 2]).then_inc(vcol_sb, 1)
            dve.wait_ge(vcol_sb, 1)
            gn_w, gn_b, bk_c, br_c = (vcol[:, i:i + 1] for i in (0, 1, 3, 4))

            def norm_mean(b):
                dve.wait_ge(ld_x[b], 16)
                for h in range(2):
                    last = nc.vector.bn_stats(gst[:, b, h, :], X[:, b, h * HALF:(h + 1) * HALF])
                link(last)
                nc.vector.bn_aggr(gmv[:, b, :], gst[:, b, :, :]).then_inc(gn_in, 1)

            def norm_variance(b):
                dve.wait_ge(gn_out, 2 * b + 1)
                gm, d = gtmp[:, b, 2:3], gtmp[:, b, 0:1]
                link(nc.vector.tensor_copy(gm, bank(GN_BANK[b])[:, 0:1]))
                link(nc.vector.tensor_tensor(d, gmv[:, b, 0:1], gm, ALU.subtract))
                nc.vector.scalar_tensor_tensor(gtmp[:, b, 1:2], d, d, gmv[:, b, 1:2], ALU.mult, ALU.add).then_inc(gn_in, 1)
                dve.wait_ge(gn_out, 2 * b + 2)
                nc.vector.tensor_scalar_add(ve[:, b, 0:1], bank(GN_BANK[b])[:, 1:2], EPS).then_inc(var_ready, 1)

            def norm_scale(b):
                dve.wait_ge(rstd_ready, b + 1)
                gm, sc = gtmp[:, b, 2:3], gtmp[:, b, 0:1]
                link(nc.vector.tensor_tensor(sc, rstd[:, b, 0:1], gn_w, ALU.mult))
                link(nc.vector.scalar_tensor_tensor(gtmp[:, b, 3:4], gm, sc, gn_b, ALU.mult, ALU.subtract))
                nc.vector.tensor_scalar(xn[:, b, :], X[:, b, :], sc, gtmp[:, b, 3:4], ALU.mult,
                                        ALU.subtract).then_inc(xn_ready, 1)

            def split(b, i):
                dve.wait_ge(hi_ready, 2 * b + i + 1)
                if i == 0:
                    nc.vector.scalar_tensor_tensor(q_lo[b][:, :], bank(4, 2), SCORE_SCALE, q_hi[b][:, :].bitcast(f32),
                                                   ALU.mult, ALU.subtract).then_inc(qk_split, 1)
                else:
                    nc.vector.tensor_tensor(k_lo[b][:, :], bank(6, 2), k_hi[b][:, :].bitcast(f32),
                                            ALU.subtract).then_inc(qk_split, 1)

            def max_slot(g):
                k, i = order[g]
                if i != "rows":
                    hd, t, h = i // (2 * QH), (i // 2) % QH, i % 2
                    dve.wait_ge(slot_ready, g + 1)
                    nc.vector.tensor_reduce(pm[:, hd, t, h:h + 1], bank(g % 2), AX, ALU.max).then_inc(slot_used, 1)
                    if i == RING - 2:
                        dve.wait_ge(slot_used, g + 1)
                        link(nc.vector.tensor_reduce(negm[:, :, :], pm[:, :, :, :], AX, ALU.max, negate=True))
                        if k:
                            dve.wait_ge(slot_ready, place[k - 1, "rows"] + 1)
                        link(nc.vector.tensor_copy(mhl[:, :, 0, :], negm[:, :, :]))
                        nc.vector.tensor_tensor(mhl[:, :, 1, :], negm[:, :, :], mhl[:, :, 0, :].bitcast(f32),
                                                ALU.subtract).then_inc(mhl_ready, 1)
                    return
                dve.wait_ge(slot_ready, g + 1)
                if k:
                    dve.wait_ge(mrow_in[k - 1], 16 * 2)
                nc.vector.tensor_copy(mrow[:, :], ps[0:4 * QH, (g % 2) * HALF:(g % 2) * HALF + P]).then_inc(mrow_ready, 1)
                dve.wait_ge(mrow_ready, k + 1)
                dve.sem_inc(slot_used, 1)

            def normalise(u, qh):
                o = 2 * u + qh
                b, pair = u // PAIRS, u % PAIRS
                dve.wait_ge(pv_done, u * STEPS + (qh + 1) * KT)
                if o:
                    dve.wait_ge(o_used, o)
                link(nc.vector.transpose(sums[:, :], bank(6 + o % 2)[64:128, :]))
                link(nc.vector.reciprocal(rec16[:, :], sums[:, :].rearrange("p (k c) -> p k c", c=32)[:, :, 0]))
                link(nc.vector.transpose(rec[:, :].rearrange("p (k c) -> p k c", c=32),
                                         rec16[:, :].unsqueeze(2).broadcast_to([64, HALF // 32, 32])))
                nc.vector.tensor_tensor(attn[64 * pair:64 * pair + 64, b, qh * HALF:(qh + 1) * HALF],
                                        bank(6 + o % 2)[0:64, :], rec[:, :], ALU.mult).then_inc(o_used, 1)

            def norm_stats(src, i):
                for j in range(J):
                    last = nc.vector.bn_stats(lst[:, j, :], src[:, j, :])
                link(last)
                for j in range(J):
                    last = nc.vector.bn_aggr(lmv[:, j, :], lst[:, j, :])
                link(last)
                nc.vector.tensor_scalar_add(ve[:, i, :], lmv[:, :, 1], EPS).then_inc(var_ready, 1)

            def norm_apply(src, dst, i, done):
                dve.wait_ge(rstd_ready, i + 1)
                for j in range(J):
                    last = nc.vector.tensor_scalar(dst[:, j, :], src[:, j, :], lmv[:, j, 0:1], rstd[:, i, j:j + 1],
                                                   ALU.subtract, ALU.mult)
                last.then_inc(done, 1)

            def v_project(b):
                dve.wait_ge(t_sb, b + 1)
                norm_stats(t2[:, b, :, :], B + 3 * b)

            def v_tokens(b):
                norm_apply(t2[:, b, :, :], F, B + 3 * b, F_ready)

            def v_key_max(b):
                dve.wait_ge(keys_ready, b + 1)
                link(nc.vector.tensor_reduce(kneg[:, 0:1], bank(0, 2), AX, ALU.max, negate=True))
                nc.vector.tensor_scalar(kneg[:, 1:2], kneg[:, 0:1], bk_c, bk_c, ALU.subtract, ALU.add).then_inc(kneg_ready, 1)

            def v_query_value(b, h):
                dve.wait_ge(qv_ready, 2 * b + h + 1)
                nc.vector.tensor_tensor(QV[:, 4 * h:4 * h + 4, :, :].rearrange("p j w k -> p j (w k)"),
                                        bank(QV_BANK[b][h], 2).rearrange("p (j k) -> p j k", j=4),
                                        bqv[:, :, :].rearrange("p w k -> p (w k)").unsqueeze(1).broadcast_to([P, 4, 2 * P]),
                                        ALU.add).then_inc(qv_sb, 1)

            def spread_query(i):
                return qst[:, :, :, i].unsqueeze(3).broadcast_to([P, J, HEADS1, HK])

            def v_query_max(b):
                dve.wait_ge(qv_sb, 2 * b + 2)
                q = QV[:, :, 0, :].rearrange("p j (h k) -> p j h k", k=HK)

                link(nc.vector.tensor_reduce(qst[:, :, :, 0], q, AX, ALU.max))
                nc.vector.tensor_tensor(q, q, spread_query(0), ALU.subtract).then_inc(qsub_ready, 1)

            def v_queries(b):
                dve.wait_ge(qexp_ready, b + 1)
                q = QV[:, :, 0, :].rearrange("p j (h k) -> p j h k", k=HK)
                link(nc.vector.tensor_reduce(qst[:, :, :, 1], q, AX, ALU.add))
                link(nc.vector.reciprocal(qst[:, :, :, 2], qst[:, :, :, 1]))

            def v_queries_scaled(b):
                q = QV[:, :, 0, :].rearrange("p j (h k) -> p j h k", k=HK)
                nc.vector.tensor_tensor(q, q, spread_query(2), ALU.mult).then_inc(qn_ready, 1)

            def v_context(b):
                dve.wait_ge(ctx_ready, b + 1)
                nc.vector.tensor_tensor(CT, ps[:, 0:P], bmask[:, :], ALU.mult).then_inc(ct_sb, 1)

            def v_fold(b):
                dve.wait_ge(ek_ready, b + 1)
                link(nc.vector.reciprocal(ksum[:, 1:2], ksum[:, 0:1]))
                dve.wait_ge(m1_ready, b + 1)
                nc.vector.tensor_scalar_mul(M1, ps[:, HALF:HALF + P], ksum[:, 1:2]).then_inc(m1_sb, 1)

            def v_attend(b):
                dve.wait_ge(att_ready, b + 1)
                t = t2[:, b, :, :].rearrange("p j c -> p (j c)")
                link(nc.vector.scalar_tensor_tensor(t, bank(0, 2), br_c, t, ALU.add, ALU.add))

            def v_stats(b):
                norm_stats(t2[:, b, :, :], B + 3 * b + 1)

            def v_norm(b):
                norm_apply(t2[:, b, :, :], F, B + 3 * b + 1, n2_ready)

            def v_stats2(b):
                dve.wait_ge(n2_ready, b + 1)
                norm_stats(F, B + 3 * b + 2)

            def v_norm2(b):
                norm_apply(F, X2[:, b, :, :], B + 3 * b + 2, x2_ready)

            def spread_gate(i):
                return lst2[:, :, i].unsqueeze(2).broadcast_to([P, J, E])

            def v_gates(b):
                dve.wait_ge(lg_ready, b + 1)
                link(nc.vector.tensor_tensor(lg[:, :, :], ps[:, 0:J * E].rearrange("p (j e) -> p j e", j=J),
                                             rb[:, :].unsqueeze(1).broadcast_to([P, J, E]), ALU.add))

                link(nc.vector.tensor_reduce(lst2[:, :, 0], lg[:, :, :], AX, ALU.max))
                nc.vector.tensor_tensor(lg[:, :, :], lg[:, :, :], spread_gate(0), ALU.subtract).then_inc(lsub_ready, 1)

            def v_route(b):
                dve.wait_ge(lexp_ready, b + 1)
                link(nc.vector.tensor_reduce(lst2[:, :, 1], lg[:, :, :], AX, ALU.add))
                link(nc.vector.reciprocal(lst2[:, :, 2], lst2[:, :, 1]))
                link(nc.vector.tensor_tensor(lg[:, :, :], lg[:, :, :], spread_gate(2), ALU.mult))
                for j in range(J):
                    last = nc.vector.max(top[:, j, :], lg[:, j, :])
                link(last)
                for j in range(J):
                    last = nc.vector.max_index(topi[:, j, :], top[:, j, :], lg[:, j, :])
                link(last)
                nc.vector.tensor_copy(topf[:, :, :], topi[:, :, 0:2])
                link(nc.vector.tensor_tensor(lst2[:, :, 3], top[:, :, 0], top[:, :, 1], ALU.add))
                link(nc.vector.reciprocal(lst2[:, :, 0], lst2[:, :, 3]))
                nc.vector.tensor_tensor(wts[:, b, :, :], top[:, :, 0:2],
                                        lst2[:, :, 0].unsqueeze(2).broadcast_to([P, J, 2]), ALU.mult)

            def v_choose(b):
                for w in range(2):
                    last = nc.vector.tensor_tensor(hot[:, w, :, :], iota_e[:, :].unsqueeze(2).broadcast_to([P, E, J]),
                                                   topf[:, :, w].unsqueeze(1).broadcast_to([P, E, J]), ALU.is_equal)
                link(last)
                nc.vector.tensor_tensor(mask[:, :, :], hot[:, 0, :, :], hot[:, 1, :, :], ALU.add).then_inc(mask_ready, 1)

            def v_slots(b):
                dve.wait_ge(cum_ready, b + 1)
                link(nc.vector.tensor_copy(tot.rearrange("p e j -> p (e j)"), ps[:, HALF + E * J:HALF + 2 * E * J]))
                link(nc.vector.tensor_tensor_scan(incl.rearrange("p e j -> p (e j)"),
                                                  seg[:, :, :].rearrange("p e j -> p (e j)"),
                                                  tot.rearrange("p e j -> p (e j)"), 0.0, ALU.mult, ALU.add))
                nc.vector.tensor_tensor(slotv, incl, tot, ALU.subtract)
                link(nc.vector.tensor_scalar_add(cnt_i[:, :], incl[:, :, J - 1], float(P - 1)))
                link(nc.vector.tensor_scalar(cnt_i[:, :], cnt_i[:, :], 7, 7, ALU.arith_shift_right, ALU.logical_shift_left))
                link(nc.vector.tensor_copy(cnt[:, 0, :], cnt_i[:, :]))
                link(nc.vector.tensor_tensor_scan(cnt[:, 1, :], ones[:, 0:E], cnt[:, 0, :], 0.0, ALU.mult, ALU.add))
                link(nc.vector.tensor_tensor(cnt[:, 2, :], cnt[:, 1, :], cnt[:, 0, :], ALU.subtract))
                link(nc.vector.tensor_tensor(slotv, slotv,
                                             cnt[:, 2, :].unsqueeze(2).broadcast_to([P, E, J]), ALU.add))
                link(nc.vector.tensor_tensor(slotv, slotv,
                                             ps[:, HALF:HALF + E * J].rearrange("p (e j) -> p e j", e=E), ALU.add))
                for w in range(2):
                    link(nc.vector.tensor_tensor(hot[:, w, :, :], hot[:, w, :, :], slotv, ALU.mult))
                    link(nc.vector.tensor_reduce(slotf[:, w, :], hot[:, w, :, :].rearrange("p e j -> p j e"), AX, ALU.add))
                nc.vector.tensor_scalar_add(slots[:, b, :, :], slotf[:, :, :], float(b * TILES * P)).then_inc(slots_ready, 1)
                link(nc.vector.tensor_tensor(cmp, t_iota[:, :, :],
                                             cnt[0:1, 1, :].unsqueeze(1).broadcast_to([1, TILES, E]), ALU.is_ge))
                link(nc.vector.tensor_reduce(tabf[:, :], cmp, AX, ALU.add))
                nc.vector.tensor_scalar_min(tab[0:1, b * TILES:(b + 1) * TILES], tabf[:, :], float(E - 1)).then_inc(tab_ready, 1)

            layer1 = {"tokens_stats": [v_project], "tokens": [v_tokens], "keys": [v_key_max],
                      "query_value0": [lambda b: v_query_value(b, 0)], "query_value1": [lambda b: v_query_value(b, 1)],
                      "keyT": [v_query_max], "queries": [v_queries], "context": [v_context], "fold": [v_fold],
                      "attend": [v_attend], "stats": [v_stats],
                      "stats2": [v_stats2], "queries_scaled": [v_queries_scaled], "choose": [v_choose],
                      "norm": [v_norm], "norm2": [v_norm2], "logits": [v_gates], "route": [v_route],
                      "counts": [v_slots]}

            norm_mean(0)
            norm_variance(0)
            norm_scale(0)
            norm_mean(1)
            split(0, 0)
            norm_variance(1)
            split(0, 1)
            norm_scale(1)
            split(1, 0)
            split(1, 1)
            dve.wait_ge(vcol_sb, 2)
            for g in range(slots_by(0)):
                max_slot(g)
            for s in range(UNITS * STEPS):
                for g in range(slots_by(s), slots_by(s + 1)):
                    max_slot(g)
                if s % KT == 1 and s > KT:
                    normalise((s // KT - 1) // 2, (s // KT - 1) % 2)
                if s == BEGIN_LAYER1:
                    dve.wait_ge(ld_rows, 16 * 4)
                    dve.wait_ge(consts_ready, 2)
                run_parts(layer1, LAYER1_AT, s, 0)
            normalise(UNITS - 1, 1)
            run_parts(layer1, LAYER1_AT_TILE, "before", 1)

            expert_of = {}

            def load_expert(s, turn):
                key = (s, isinstance(turn, int))
                if key not in expert_of:
                    if s in (0, TILES):
                        dve.wait_ge(tab_ready, s // TILES + 1)
                    expert_of[key] = dve.value_load(tab[0:1, bass.ds(s + STRIDE * turn, 1)], min_val=0, max_val=E - 1)
                return expert_of[key]

            def x_copy(s, turn):
                n = s + STRIDE * turn
                e = load_expert(s, turn)
                dve.wait_ge(xT_ready, n + 1)
                nc.vector.tensor_scalar(XTT[:, s % NB, :], bank(6 + s % 2)[:, P:2 * P], vcol[:, bass.ds(e + 5, 1)],
                                        vcol[:, bass.ds(e + (5 + E), 1)], ALU.mult, ALU.add).then_inc(xT_sb, 1)

            def expert_step(s, turn):
                n = s + STRIDE * turn
                if s == 0:
                    x_copy(0, 0)
                    x_copy(1, 0)
                if is_tile(s):
                    e = load_expert(s, turn)
                    if is_tile(s + 2):
                        load_expert(s + 2, turn)
                    dve.wait_ge(h_ready, n + 1)
                    if s >= NB:
                        dve.wait_ge(g_ready, n - 2)
                    nc.vector.tensor_tensor(H1[:, s % NB, :], bank(2 + s % 2), bias1[:, e, :], ALU.add).then_inc(h_sb, 1)
                if is_tile(s + 2):
                    x_copy(s + 2, turn)
                if is_tile(s - 3):
                    t = s - 3
                    e = load_expert(t, turn)
                    dve.wait_ge(y_ready, n - 2)
                    if t >= NB:
                        dve.wait_ge(y_out[t % NB], 16 * (t // NB + STRIDE // NB * turn))
                    nc.vector.tensor_tensor(Y[:, t % NB, :], bank(6 + t % 2)[:, 0:D], bias2[:, e, :],
                                            ALU.add).then_inc(y_sb, 1)

            dve.wait_ge(ld_b1, 16)
            dve.wait_ge(ld_b2, 16)
            expert_steps(dve, expert_step, layer1)
            for b in range(B):
                for g in range(GROUPS):
                    dve.wait_ge(gathered[b][g], 16 * 4)
                    for w in range(2):
                        for j in (2 * g, 2 * g + 1):
                            t = t2[:, b, j, :]
                            last = nc.vector.scalar_tensor_tensor(t, YG[:, b, 2 * j + w, :], wts[:, b, j, w:w + 1], t,
                                                                  ALU.mult, ALU.add)
                        if w == 0:
                            link(last)
                    last.then_inc(mix_ready, 1)


_INS = ['x', 'L0_conv_gn_weight', 'L0_conv_gn_bias', 'L0_conv_qkv_weight', 'L0_conv_out_weight', 'L0_conv_out_bias',
        'L1_attn_Wk', 'L1_attn_bk', 'L1_attn_Wq', 'L1_attn_bq', 'L1_attn_Wv', 'L1_attn_bv', 'L1_attn_Wr', 'L1_attn_br',
        'L1_ffn_Wr', 'L1_ffn_br', 'L1_ffn_ln_g', 'L1_ffn_ln_b', 'L1_ffn_W1', 'L1_ffn_b1', 'L1_ffn_W2', 'L1_ffn_b2']
_OUT = ((2, 128, 32, 32), 'float32')


def kernel(**inputs):
    import numpy as _np
    import concourse.bacc as _bacc
    from concourse import mybir as _mybir
    from concourse.bass_utils import run_bass_kernel_spmd as _run

    nc = _bacc.Bacc("TRN2", target_bir_lowering=False, num_devices=1)
    arrays, args = {}, []
    for name in _INS:
        a = _np.ascontiguousarray(inputs[name])
        arrays[f"in_{name}"] = a
        args.append(nc.dram_tensor(f"in_{name}", a.shape, _mybir.dt.from_np(a.dtype), kind="ExternalInput").ap())
    shape, dtype = _OUT
    args.append(nc.dram_tensor("out_0", shape, _mybir.dt.from_np(_np.dtype(dtype)), kind="ExternalOutput").ap())
    build_program(nc, *args)
    r = _run(nc, [arrays], core_ids=[0])
    return r.results[0]["out_0"]
```
